# Optimizing a Trainium2 kernel written in Bass

```python
import numpy as np
import jax
import jax.numpy as jnp

def _softmax(x, axis=-1):
    return jax.nn.softmax(x, axis=axis)

def _gelu(x):
    return jax.nn.gelu(x, approximate=True)

def _silu(x):
    return jax.nn.silu(x)

def _sigmoid(x):
    return jax.nn.sigmoid(x)

def _layernorm(x, axis=-1, eps=1e-05):
    m = jnp.mean(x, axis=axis, keepdims=True)
    v = jnp.var(x, axis=axis, keepdims=True)
    return (x - m) / jnp.sqrt(v + eps)

def _scatter_add(tgt, idx, src, axis=0):
    return tgt.at[idx].add(src)

def _segment_sum(src, seg, n):
    return jax.ops.segment_sum(src, seg, n)
kernel_name = 'mk_flamingo_gated_d1_seqx_r4_ba3ac8'

def setup_inputs(seed: int=0):
    np.random.seed(seed)
    _w = jnp.asarray

    def _rec_inputs():
        import jax
        import jax.numpy as jnp
        _rk = jax.random.key(seed)
        x = -0.0002928 + 1 * jax.random.normal(jax.random.fold_in(_rk, 1), (32, 128, 512), jnp.float32)
        _lenS = 128 - jax.random.randint(jax.random.fold_in(_rk, 7), (32,), 0, max(1, 128 // 4) + 1, jnp.int32)
        _lenS2 = 128 - jax.random.randint(jax.random.fold_in(_rk, 8), (32,), 0, max(1, 128 // 4) + 1, jnp.int32)
        _ctx_2048P = jax.random.normal(jax.random.fold_in(_rk, 11), (32, 16, 512), jnp.float32)
        _ctx_2048c = jax.random.dirichlet(jax.random.fold_in(_rk, 511), 0.3 * jnp.ones((16,), jnp.float32), (32, 128))
        _ctx_2048t = jnp.einsum('bsk,bkd->bsd', _ctx_2048c, _ctx_2048P)
        _ctx_2048t = _ctx_2048t * jax.lax.rsqrt(jnp.mean(jnp.square(_ctx_2048t)) + 1e-12) * 0.953939
        ctx_2048 = -1.39393e-06 + 0.999914 * (_ctx_2048t + 0.3 * jax.random.normal(jax.random.fold_in(_rk, 611), (32, 128, 512), jnp.float32))
        _g = jax.random.normal(jax.random.fold_in(_rk, 9001), (2, 1), jnp.float32)
        _g = jnp.sign(_g) * jnp.maximum(jnp.abs(_g), 1.0) + (_g == 0) * 1.0
        g_xattn = _g[0]
        g_ffn = _g[1]
        return (x, ctx_2048, g_xattn, g_ffn)
    x, ctx_2048, g_xattn, g_ffn = _rec_inputs()

    def _L0_xattn_setup():
        import jax, jax.numpy as jnp
        import numpy as np
        H = 8
        D_MODEL = 128
        D_HEAD = D_MODEL // H
        key = jax.random.key(seed)
        ks = jax.random.split(key, 8)
        B, C, L = (4, D_MODEL, 512)
        s = 1.0 / np.sqrt(D_MODEL)
        return {'x1': jax.random.normal(ks[0], (B, C, L), dtype=jnp.float32), 'x2': jax.random.normal(ks[1], (B, C, L), dtype=jnp.float32), 'Wq': jax.random.uniform(ks[2], (D_MODEL, D_MODEL), jnp.float32, -s, s), 'bq': jax.random.uniform(ks[3], (D_MODEL,), jnp.float32, -s, s), 'Wk': jax.random.uniform(ks[4], (D_MODEL, D_MODEL), jnp.float32, -s, s), 'bk': jax.random.uniform(ks[5], (D_MODEL,), jnp.float32, -s, s), 'Wv': jax.random.uniform(ks[6], (D_MODEL, D_MODEL), jnp.float32, -s, s), 'bv': jax.random.uniform(ks[7], (D_MODEL,), jnp.float32, -s, s)}
    _L0_xattn_all = _L0_xattn_setup()
    _L0_xattn_in = {k: v for k, v in _L0_xattn_all.items() if k in ('Wq', 'bq', 'Wk', 'bk', 'Wv', 'bv')}
    del _L0_xattn_all

    def _L0_ffn_setup():
        import jax, jax.numpy as jnp
        import numpy as np
        B, S, D = (4, 512, 512)
        E, F, K = (8, 256, 2)
        SF = 256
        EPS = 1e-06

        def _rmsnorm(x, w, eps=EPS):
            var = jnp.mean(x * x, axis=-1, keepdims=True)
            return x * jax.lax.rsqrt(var + eps) * w
        key = jax.random.key(seed)
        ks = jax.random.split(key, 9)
        g = lambda k, shape, scale: jax.random.normal(k, shape, jnp.float32) * scale
        return {'x': g(ks[0], (B, S, D), 1.0), 'rms_weight': jnp.ones((D,), jnp.float32), 'router_w': g(ks[1], (D, E), 0.02), 'w_gate': g(ks[2], (E, D, F), 0.02), 'w_up': g(ks[3], (E, D, F), 0.02), 'w_down': g(ks[4], (E, F, D), 0.02), 'sw_gate': g(ks[5], (D, SF), 0.02), 'sw_up': g(ks[6], (D, SF), 0.02), 'sw_down': g(ks[7], (SF, D), 0.02)}
    _L0_ffn_all = _L0_ffn_setup()
    _L0_ffn_in = {k: v for k, v in _L0_ffn_all.items() if k in ('rms_weight', 'router_w', 'w_gate', 'w_up', 'w_down', 'sw_gate', 'sw_up', 'sw_down')}
    del _L0_ffn_all
    return {'x': x, 'ctx_2048': ctx_2048, 'g_xattn': g_xattn, 'g_ffn': g_ffn, 'L0_xattn_Wq': _L0_xattn_in['Wq'], 'L0_xattn_bq': _L0_xattn_in['bq'], 'L0_xattn_Wk': _L0_xattn_in['Wk'], 'L0_xattn_bk': _L0_xattn_in['bk'], 'L0_xattn_Wv': _L0_xattn_in['Wv'], 'L0_xattn_bv': _L0_xattn_in['bv'], 'L0_ffn_rms_weight': _L0_ffn_in['rms_weight'], 'L0_ffn_router_w': _L0_ffn_in['router_w'], 'L0_ffn_w_gate': _L0_ffn_in['w_gate'], 'L0_ffn_w_up': _L0_ffn_in['w_up'], 'L0_ffn_w_down': _L0_ffn_in['w_down'], 'L0_ffn_sw_gate': _L0_ffn_in['sw_gate'], 'L0_ffn_sw_up': _L0_ffn_in['sw_up'], 'L0_ffn_sw_down': _L0_ffn_in['sw_down']}

def reference(x, ctx_2048, g_xattn, g_ffn, L0_xattn_Wq, L0_xattn_bq, L0_xattn_Wk, L0_xattn_bk, L0_xattn_Wv, L0_xattn_bv, L0_ffn_rms_weight, L0_ffn_router_w, L0_ffn_w_gate, L0_ffn_w_up, L0_ffn_w_down, L0_ffn_sw_gate, L0_ffn_sw_up, L0_ffn_sw_down):
    import jax
    import jax.numpy as jnp

    def _L0_xattn_ref(x1, x2, Wq, bq, Wk, bk, Wv, bv):
        import jax, jax.numpy as jnp
        import numpy as np
        H = 8
        D_MODEL = 128
        D_HEAD = D_MODEL // H
        B, C, L = x1.shape
        x1t = jnp.swapaxes(x1, 1, 2)
        x2t = jnp.swapaxes(x2, 1, 2)

        def proj(x, W, b):
            y = jnp.einsum('blc,dc->bld', x, W) + b
            return y.reshape(B, -1, H, D_HEAD).transpose(0, 2, 1, 3)
        q = proj(x1t, Wq, bq)
        k = proj(x2t, Wk, bk)
        v = proj(x2t, Wv, bv)
        scores = jnp.einsum('bhqd,bhkd->bhqk', q, k) / jnp.sqrt(jnp.asarray(D_HEAD, dtype=q.dtype))
        attn = jax.nn.softmax(scores, axis=-1)
        out = jnp.einsum('bhqk,bhkd->bhqd', attn, v)
        out = out.transpose(0, 2, 1, 3).reshape(B, L, C)
        return jnp.swapaxes(out, 1, 2)

    def _L0_ffn_ref(x, rms_weight, router_w, w_gate, w_up, w_down, sw_gate, sw_up, sw_down):
        import jax, jax.numpy as jnp
        import numpy as np
        B, S, D = (4, 512, 512)
        E, F, K = (8, 256, 2)
        SF = 256
        EPS = 1e-06

        def _rmsnorm(x, w, eps=EPS):
            var = jnp.mean(x * x, axis=-1, keepdims=True)
            return x * jax.lax.rsqrt(var + eps) * w
        b, s, d = x.shape
        e = router_w.shape[1]
        h = _rmsnorm(x, rms_weight)
        ht = h.reshape(-1, d)
        t = ht.shape[0]
        logits = ht @ router_w
        probs = jax.nn.softmax(logits, axis=-1)
        topv, topi = jax.lax.top_k(probs, K)
        topv = topv / jnp.sum(topv, axis=-1, keepdims=True)
        w_dense = jnp.zeros((t, e), ht.dtype).at[jnp.arange(t)[:, None], topi].set(topv)
        g = jnp.einsum('td,edf->tef', ht, w_gate)
        u = jnp.einsum('td,edf->tef', ht, w_up)
        eo = jnp.einsum('tef,efd->ted', jax.nn.silu(g) * u, w_down)
        moe = jnp.einsum('te,ted->td', w_dense, eo)
        sh = jax.nn.silu(ht @ sw_gate) * (ht @ sw_up) @ sw_down
        return (moe + sh).reshape(b, s, d)
    x = x + jnp.tanh(g_xattn[0]) * _L0_xattn_ref(_layernorm(x, axis=-1), ctx_2048, L0_xattn_Wq, L0_xattn_bq, L0_xattn_Wk, L0_xattn_bk, L0_xattn_Wv, L0_xattn_bv)
    x = x + jnp.tanh(g_ffn[0]) * _L0_ffn_ref(_layernorm(x, axis=-1), L0_ffn_rms_weight, L0_ffn_router_w, L0_ffn_w_gate, L0_ffn_w_up, L0_ffn_w_down, L0_ffn_sw_gate, L0_ffn_sw_up, L0_ffn_sw_down)
    return x

_drawn_inputs = setup_inputs


def setup_inputs(seed=0):
    import zlib

    import numpy as np

    out = dict(_drawn_inputs(seed))
    spreads = {'L0_ffn_rms_weight': (1.0, 0.6)}
    factors = {'L0_xattn_bq': 8.0, 'L0_xattn_bk': 8.0}
    for name, (base, spread) in spreads.items():
        noise = np.random.default_rng([zlib.crc32(name.encode()), seed]).standard_normal(out[name].shape)
        drawn = base * np.exp(spread * noise) if base else spread * noise
        out[name] = jnp.asarray(drawn.astype(out[name].dtype))
    for name, factor in factors.items():
        out[name] = (out[name] * factor).astype(out[name].dtype)
    return out
```

```python
from contextlib import ExitStack

import concourse.bass as bass
from concourse import mybir

F32 = mybir.dt.float32
BF16 = mybir.dt.bfloat16
ALU = mybir.AluOpType
ACT = mybir.ActivationFunctionType
I32 = mybir.dt.int32
AX_X = mybir.AxisListType.X

P = 128
HEADS = 8
DH = P // HEADS
L = 512
KT = L // P
LN_EPS = 1e-5
RMS_EPS = 1e-6
DMA = 16

HI, MID, LO = range(3)
K_PARTS = (HI, MID, LO, HI, MID, HI)
Q_PARTS = (HI, HI, HI, MID, MID, LO)


def runs(parts):
    out = []
    for at, part in enumerate(parts):
        if out and part == out[-1][1] + out[-1][2]:
            out[-1][2] += 1
        else:
            out.append([at, part, 1])
    return out


READS = len(runs(K_PARTS)) + len(runs(Q_PARTS))
STACK = len(K_PARTS) * DH
SHIFTED = STACK + 2

STEPS = HEADS * KT
PROJECT_AT = {21: (3, 0), 24: (3, 1), 7: (2, 2)}
EVAC_AT = {22: (3, 0), 25: (3, 1), 8: (2, 2)}
MAX_AT = (18, 2)
VALUES_LATE = 2
RECIP_AT = 13
ROW_AT = (24, 9)
GROUP = 4
EXPERTS = 8
FF = 256
CHUNKS = L // P
IN_RING, OUT_RING = 5, 3
ARENA = 33280
W_ROWS = CHUNKS + FF // P
LN_FIRST = 5


class Arena:

    def __init__(self, tensor, start=0):
        self.tensor, self.at = tensor, start

    def take(self, words, dtype=F32):
        view = self.tensor[:, self.at:self.at + words]
        self.at += words
        return view if dtype == F32 else view.bitcast(dtype)


def build(nc, x_d, ctx_d, g_xattn_d, g_ffn_d, wq_d, bq_d, wk_d, bk_d, wv_d, bv_d, rms_d, router_d, w_d, out_d):
    B = x_d.shape[0]
    T = B * P
    NT = 2 * B + EXPERTS - 1
    es = ExitStack()
    with es:
        def sem(name):
            return es.enter_context(nc.semaphore(name))

        def sb(name, shape, dt=F32):
            return es.enter_context(nc.sbuf_tensor(name, shape, dt))

        def psum(name, shape, dt=F32):
            return es.enter_context(nc.psum_tensor(name, shape, dt))

        def dram(name, shape, dt):
            return nc.dram_tensor(name, shape, dt, kind="Internal").ap()

        xs = sb("xs", [P, B, L])
        arena = sb("arena", [P, ARENA])
        a = Arena(arena)
        q_stack = [a.take(HEADS * L // 2, BF16).rearrange("p (h l) -> p h l", h=HEADS) for _ in range(3)]
        k_stack = [a.take(HEADS * L // 2, BF16).rearrange("p (h l) -> p h l", h=HEADS) for _ in range(3)]
        probs = [a.take(GROUP * L).rearrange("p (j l) -> p j l", j=GROUP) for _ in range(3)]
        v_ones = [a.take(KT * HEADS * 2 * DH).rearrange("p (t h e) -> p t h e", t=KT, h=HEADS) for _ in range(3)]
        ctx_in = [a.take(L) for _ in range(2)]
        xn = [a.take(L) for _ in range(2)]
        proj = [a.take(L) for _ in range(2)]
        rest = a.take(L)
        parts = [[a.take(L // 2, BF16) for _ in range(3)] for _ in range(2)]
        pv_sb = a.take(2 * L).rearrange("p (g l) -> p g l", g=2)
        pv_num = a.take(L)
        pv_rden = a.take(L)
        attn = a.take(L)
        den_c = a.take(L * HEADS // P)
        rden_c = a.take(L * HEADS // P)
        wq, wk, wv = (a.take(P) for _ in range(3))
        attention_end = a.at

        a = Arena(arena)
        w_routed = a.take(EXPERTS * W_ROWS * L).rearrange("p (e r n) -> p e r n", e=EXPERTS, r=W_ROWS)
        hidden = [a.take(FF) for _ in range(2)]
        act = [a.take(FF) for _ in range(2)]
        act_t = [a.take(FF).rearrange("p (c n) -> p c n", c=FF // P) for _ in range(2)]
        h_t = [a.take(L).rearrange("p (c n) -> p c n", c=CHUNKS) for _ in range(3)]
        h_in = [a.take(L) for _ in range(3)]
        gathered = [xs[:, n, :] for n in range(IN_RING)]
        y_sb = [xs[:, IN_RING + n, :] for n in range(OUT_RING)]
        a = Arena(arena, max(a.at, attention_end))
        w_shared = a.take(W_ROWS * L).rearrange("p (r n) -> p r n", r=W_ROWS)
        w_rms = a.take(L)
        assert a.at <= ARENA, a.at
        R = B * EXPERTS
        a = Arena(w_routed[:, EXPERTS - 1].rearrange("p r n -> p (r n)"))

        def by_token(v):
            return v.rearrange("p (t e) -> p t e", e=EXPERTS)

        def by_expert(v):
            return v.rearrange("p (e t) -> p e t", e=EXPERTS)

        prob = a.take(R)
        left = a.take(R)
        pick = [a.take(R) for _ in range(2)]
        rank = a.take(R)
        r_i = a.take(R, F32)
        r_tmp = a.take(R)
        place = a.take(R)
        restart = a.take(R)
        le = a.take(NT * EXPERTS)

        bias = sb("bias", [P, 3])
        gates = sb("gates", [P, 2])
        tgates = sb("tgates", [P, 2])
        tg_bv = sb("tg_bv", [P, 1])
        ident = sb("ident", [P, P])
        stats = sb("stats", [P, B, 6])
        mv = sb("mv", [P, B, 2])
        std = sb("std", [P, B])
        rstd = sb("rstd", [P, B])
        nmr = sb("nmr", [P, B])
        row_max = [sb(f"row_max{i}", [P, HEADS * KT]) for i in range(2)]
        m_rows = [sb(f"m_rows{i}", [GROUP * KT, 2, P], BF16) for i in range(2)]

        mv2 = sb("mv2", [P, B, 2])
        r2 = sb("r2", [P, B])
        nmr2 = sb("nmr2", [P, B])
        r2a = sb("r2a", [P, B])
        w_router = sb("w_router", [P, CHUNKS, EXPERTS])
        before = sb("before", [P, P], BF16)
        ones = sb("ones", [P, P], BF16)
        top = sb("top", [P, 8, B])
        chosen = sb("chosen", [P, R], BF16)
        slots = sb("slots", [P, 2, B], I32)
        meta = sb("meta", [P, 2, B, 2])
        per_e = sb("per_e", [P, 4, EXPERTS])
        per_ei = sb("per_ei", [P, EXPERTS], I32)
        slot_map = sb("slot_map", [NT, P, 2])
        slot_i = sb("slot_i", [P, P], I32)
        ids = sb("ids", [P, NT], I32)
        wts = sb("wts", [P, NT])
        expert_of = sb("expert_of", [P, NT], I32)
        tile_no = sb("tile_no", [P, NT])

        banks = [psum(f"bank{i}", [P, L]) for i in range(8)]
        E_BANKS, M_BANKS = 3, 3
        e_ps = banks[0:E_BANKS]
        m_ps = banks[E_BANKS:E_BANKS + M_BANKS]
        pv_ps, misc_ps = banks[6:8]

        parts_d = [[dram(f"parts_{n}{i}", (HEADS, 3, DH, L), BF16) for i in range(2)] for n in "qk"]
        pv_d = dram("pv_d", (HEADS, 2 * DH, L), F32)
        rden_d = dram("rden_d", (HEADS, L), F32)
        h_d = dram("h_d", (T + P, L), F32)
        ht_d = dram("ht_d", (B, P, L), F32)
        map_d = dram("map_d", (NT * P, 2), F32)

        s_const = sem("s_const")
        s_setup = sem("s_setup")
        s_ones = sem("s_ones")
        XCH = 4
        s_x = [sem(f"s_xin{i}") for i in range((B + XCH - 1) // XCH)]
        s_ctx = [sem(f"s_ctx{i}") for i in range(2)]
        s_dve = sem("s_dve")
        s_var = sem("s_var")
        s_std = sem("s_std")
        s_rstd = sem("s_rstd")
        s_tanh = sem("s_tanh")
        s_gate = sem("s_gate")
        s_pool = sem("s_pool")
        s_xn = sem("s_xn")
        s_proj = sem("s_proj")
        s_evac = sem("s_evac")
        s_part = sem("s_part")
        s_wr = [sem(f"s_wr{i}") for i in range(2)]
        s_rd = [sem(f"s_rd{i}") for i in range(3)]
        s_ms = sem("s_ms")
        s_mx = sem("s_mx")
        s_mt = sem("s_mt")
        s_mr = sem("s_mr")
        s_row = [sem(f"s_row{i}") for i in range(2)]
        s_es = sem("s_es")
        s_exp = sem("s_exp")
        s_pv = sem("s_pv")
        s_u = sem("s_u")
        s_w = sem("s_w")
        s_sc = sem("s_sc")
        s_rc = sem("s_rc")
        s_r = sem("s_r")
        s_fin = sem("s_fin")
        s_x2 = sem("s_x2")
        s_wsh = sem("s_wsh")
        s_wrt = sem("s_wrt")
        s_var2 = sem("s_var2")
        s_std2 = sem("s_std2")
        s_h = sem("s_h")
        s_hst = [sem(f"s_hst{i}") for i in range(3)]
        s_pad = sem("s_pad")
        s_tr = sem("s_tr")
        s_hf = sem("s_hf")
        s_hts = [sem(f"s_hts{i}") for i in range(3)]
        s_lg = sem("s_lg")
        s_el = sem("s_el")
        s_ex = sem("s_ex")
        s_ch = sem("s_ch")
        s_cnt = sem("s_cnt")
        s_iota = sem("s_iota")
        s_cc = sem("s_cc")
        s_map0 = sem("s_map0")
        s_slot = sem("s_slot")
        s_eid = sem("s_eid")
        s_sc2 = sem("s_sc2")
        s_map = sem("s_map")
        s_mtr = sem("s_mtr")
        s_ids = sem("s_ids")
        s_src = [sem(f"s_src{i}") for i in range(3)]
        s_got = [sem(f"s_got{i}") for i in range(IN_RING)]
        s_hr = sem("s_hr")
        s_gu = sem("s_gu")
        s_si = sem("s_si")
        s_a = sem("s_a")
        s_ta = sem("s_ta")
        s_at = sem("s_at")
        s_dn = sem("s_dn")
        s_ysh = sem("s_ysh")
        s_yrt = sem("s_yrt")
        s_res = [sem(f"s_res{i}") for i in range(2)]
        s_acc = sem("s_acc")

        G_PS = banks[0:2]
        Y_PS = banks[2:4]
        T_PS = banks[4:6]
        A_PS = banks[6]
        R_PS = banks[7]
        JOBS = B + NT
        LATE_AT = min(14, max(B - 5, 0))
        MAP_AT = max(B - 6, 0)
        TURN_AT = max(B - 4, 1)

        chunks = [(0, min(LN_FIRST, B))] + ([(LN_FIRST, B)] if B > LN_FIRST else [])
        n_const = 8
        TURNS = range(-3, B + 2)

        def is_b(b):
            return 0 <= b < B

        block = es.enter_context(nc.Block())

        @block.sync
        def _(sp):
            def load(dst, src):
                sp.dma_start(dst, src).then_inc(s_const, DMA)

            def load_x(n):
                b0, b1 = n * XCH, min((n + 1) * XCH, B)
                sp.dma_start(xs[:, b0:b1, :], x_d[b0:b1].rearrange("b c l -> c b l")).then_inc(s_x[n], DMA)

            def load_ctx(b):
                if b >= 2:
                    sp.wait_ge(s_proj, 3 * (b - 2) + 3)
                sp.dma_start(ctx_in[b % 2], ctx_d[b]).then_inc(s_ctx[b % 2], DMA)

            load_x(0)
            load(wq[:], wq_d)
            load(wk[:], wk_d)
            load_ctx(0)
            load(wv[:], wv_d)
            load(gates[:, 0:1], g_xattn_d.broadcast_to([P, 1]))
            load(gates[:, 1:2], g_ffn_d.broadcast_to([P, 1]))
            for n, v in enumerate((bq_d, bk_d, bv_d)):
                load(bias[:, n:n + 1], v)
            if B > 1:
                load_ctx(1)
            for n in range(1, len(s_x)):
                load_x(n)

            for i in TURNS:
                done = i - 1
                new, newer = i + 2, i + 3

                def write(b, n, part):
                    if b >= 2 and part == 0:
                        sp.wait_ge(s_rd[(b - 2) % 3], READS * DMA * ((b - 2) // 3 + 1))
                    sp.wait_ge(s_part, 6 * b + 3 * n + part + 1)
                    sp.dma_start(parts_d[n][b % 2][:, part, :, :], parts[n][part]).then_inc(s_wr[n], DMA)

                def read(b, n):
                    sp.wait_ge(s_wr[n], 3 * DMA * (b + 1))
                    if b >= 3 and n == 0:
                        sp.wait_ge(s_es, STEPS * (b - 2))
                    src = parts_d[n][b % 2]
                    stack = (q_stack, k_stack)[n][b % 3]
                    order = (Q_PARTS, K_PARTS)[n]
                    for at, part, k in runs(order):
                        sp.dma_start(stack[at * DH:(at + k) * DH, :, :],
                                     src[:, part:part + k].rearrange("h t d l -> (t d) h l")
                                     ).then_inc(s_rd[b % 3], DMA)

                if is_b(new):
                    read(new, 0)
                if is_b(done):
                    sp.wait_ge(s_u, 2 * done + 2)
                    sp.wait_ge(s_fin, 2 * DMA * done)
                    sp.dma_start(pv_d.rearrange("(g h) e l -> (h e) g l", g=2), pv_sb).then_inc(s_w, DMA)
                if is_b(new):
                    write(new, 1, HI)
                if is_b(done):
                    sp.wait_ge(s_w, DMA * (done + 1))
                    if done:
                        sp.wait_ge(s_rc, done)
                    sp.dma_start(den_c, pv_d[:, DH, :].rearrange("h (c w) -> h c w", c=DH)).then_inc(s_sc, DMA)
                if is_b(new):
                    write(new, 1, MID)
                if is_b(done):
                    sp.wait_ge(s_rc, done + 1)
                    sp.dma_start(rden_d, rden_c).then_inc(s_r, DMA)
                if is_b(new):
                    write(new, 1, LO)
                if is_b(i + 4) and i + 4 >= 2:
                    load_ctx(i + 4)
                if is_b(new):
                    read(new, 1)
                if is_b(done):
                    sp.wait_ge(s_r, DMA * (done + 1))
                    if done:
                        sp.wait_ge(s_x2, done)
                    sp.dma_start(pv_rden, rden_d.unsqueeze(1).broadcast_to([HEADS, DH, L])).then_inc(s_fin, DMA)
                    sp.dma_start(pv_num, pv_d[:, 0:DH, :]).then_inc(s_fin, DMA)
                if is_b(newer):
                    for part in (HI, MID, LO):
                        write(newer, 0, part)

            sp.dma_start(w_router[:], router_d.rearrange("(c p) e -> p c e", p=P)).then_inc(s_pad, DMA)
            sp.dma_start(w_rms, rms_d.broadcast_to([P, L])).then_inc(s_pad, DMA)
            sp.dma_start(w_shared, w_d[0]).then_inc(s_wsh, DMA)

            def load_expert(e):
                sp.dma_start(w_routed[:, e], w_d[1 + e]).then_inc(s_wrt, DMA)

            sp.wait_ge(s_x2, B)
            experts = list(range(EXPERTS - 1))
            for t in range(B + 1):
                if t < B:
                    sp.wait_ge(s_h, t + 1)
                    sp.dma_start(h_d[t * P:(t + 1) * P, :], h_in[t % 3]).then_inc(s_hst[t % 3], DMA)
                if t == 0:
                    sp.dma_start(h_d[T:T + P, :], h_in[0]).then_inc(s_hst[0], DMA)
                if t >= 1:
                    sp.wait_ge(s_hf, t)
                    sp.dma_start(ht_d[t - 1], h_t[(t - 1) % 3]).then_inc(s_hts[(t - 1) % 3], DMA)
                if t % 4 == 3 and experts:
                    load_expert(experts.pop(0))
            while experts:
                load_expert(experts.pop(0))

            def source(j):
                if j < 3:
                    sp.wait_ge(s_lg, B)
                    for n in range(3):
                        sp.wait_ge(s_hts[n], DMA * len(range(n, B, 3)))
                else:
                    sp.wait_ge(s_gu, j - 2)
                sp.dma_start(h_t[j % 3], ht_d[j]).then_inc(s_src[j % 3], DMA)

            for j in range(B + 3):
                if j < B:
                    source(j)
                if j == 2:
                    sp.wait_ge(s_cc, 1)
                    sp.dma_start(map_d.rearrange("(n s) k -> n s k", s=P), slot_map[:]).then_inc(s_map0, DMA)
                if j == LATE_AT:
                    sp.wait_ge(s_eid, 1)
                    load_expert(EXPERTS - 1)
                if j == MAP_AT:
                    sp.wait_ge(s_sc2, 2 * B * DMA)
                    sp.dma_start(slot_map[:], map_d.rearrange("(n s) k -> n s k", s=P)).then_inc(s_map, DMA)
                if j >= 3:
                    sp.wait_ge(s_ysh, j - 2)
                    sp.dma_start(out_d[(j - 3) * P:(j - 2) * P, :], xs[:, j - 3, :]
                                 ).then_inc(s_res[j - 3 >= IN_RING + OUT_RING], DMA)
                if j == 3:
                    sp.dma_start(out_d[T:T + P, :], xs[:, 0, :]).then_inc(s_res[0], DMA)
            sp.wait_ge(s_acc, NT * DMA)

        @block.gpsimd
        def _(pool):
            links = [0]

            def link(ins):
                links[0] += 1
                ins.then_inc(s_pool, 1)
                pool.wait_ge(s_pool, links[0])

            link(nc.gpsimd.memset(ident[:], 0.0))
            nc.gpsimd.affine_select(out=ident[:], in_=ident[:], compare_op=ALU.not_equal, fill=1.0, base=0,
                                    pattern=[[-1, P]], channel_multiplier=1).then_inc(s_setup, 1)

            def normalise(b):
                pool.wait_ge(s_rstd, 1 if b < LN_FIRST else 2)
                if b >= 2:
                    pool.wait_ge(s_proj, 3 * (b - 2) + 2)
                nc.gpsimd.tensor_scalar(xn[b % 2], xs[:, b, :], rstd[:, b:b + 1], nmr[:, b:b + 1],
                                        ALU.mult, ALU.add).then_inc(s_xn, 1)

            def split(b, n):
                pool.wait_ge(s_evac, 3 * b + n + 1)
                if b:
                    pool.wait_ge(s_wr[n], 3 * DMA * b)
                hi, mid, lo = parts[n]

                def both(ins):
                    ins.then_inc(s_part, 1)
                    return ins

                both(nc.gpsimd.tensor_scalar(hi, proj[n], 1.0, None, ALU.mult))
                pool.wait_ge(s_part, 6 * b + 3 * n + 1)
                link(nc.gpsimd.tensor_tensor(rest, proj[n], hi, ALU.subtract))
                both(nc.gpsimd.tensor_scalar(mid, rest, 1.0, None, ALU.mult))
                pool.wait_ge(s_part, 6 * b + 3 * n + 2)
                both(nc.gpsimd.tensor_tensor(lo, rest, mid, ALU.subtract))
                pool.wait_ge(s_part, 6 * b + 3 * n + 3)

            def add_attention(b):
                pool.wait_ge(s_fin, 2 * DMA * (b + 1))
                if b == 0:
                    pool.wait_ge(s_gate, 1)
                link(nc.gpsimd.tensor_tensor(attn, pv_num, pv_rden, ALU.mult))
                link(nc.gpsimd.tensor_scalar(attn, attn, tgates[:, 0:1], tg_bv[:], ALU.mult, ALU.add))
                nc.gpsimd.tensor_tensor(xs[:, b, :], xs[:, b, :], attn, ALU.add).then_inc(s_x2, 1)
                pool.wait_ge(s_x2, b + 1)

            link(nc.gpsimd.memset(before[:], 1.0))
            nc.gpsimd.affine_select(out=before[:], in_=before[:], compare_op=ALU.is_gt, fill=0.0, base=0,
                                    pattern=[[1, P]], channel_multiplier=-1).then_inc(s_setup, 1)
            nc.gpsimd.memset(ones[:], 1.0).then_inc(s_setup, 1)
            nc.gpsimd.iota(slot_i[:], pattern=[[1, P]], base=T, channel_multiplier=0).then_inc(s_setup, 1)

            normalise(0)
            for i in TURNS:
                if is_b(i + 2):
                    split(i + 2, 1)
                if is_b(i + 4):
                    normalise(i + 4)
                if is_b(i + 3):
                    split(i + 3, 0)
                if is_b(i - 1):
                    add_attention(i - 1)

            for out, pattern, base, cm in (
                    (by_token(rank), [[0, B], [-1, EXPERTS]], EXPERTS, 0),
                    (tile_no[:], [[1, NT]], 0, 0),
                    (top[:, 7, :], [[P, B]], 0, 1)):
                nc.gpsimd.iota(out.bitcast(I32), pattern=pattern, base=base, channel_multiplier=cm).then_inc(s_iota, 1)

            pool.wait_ge(s_slot, 1)
            pool.wait_ge(s_map0, DMA)
            for k in range(2):
                for t in range(B):
                    nc.gpsimd.indirect_dma_start(
                        map_d, bass.IndirectOffsetOnAxis(ap=slots[:, k, t:t + 1], axis=0),
                        meta[:, k, t, :], None).then_inc(s_sc2, DMA)
            def gather(i):
                if i >= IN_RING:
                    pool.wait_ge(s_tr, B + i - IN_RING + 1)
                nc.gpsimd.indirect_dma_start(gathered[i % IN_RING], None, h_d,
                                             bass.IndirectOffsetOnAxis(ap=ids[:, i:i + 1], axis=0)
                                             ).then_inc(s_got[i % IN_RING], DMA)

            def add_to_output(i):
                pool.wait_ge(s_yrt, i + 1)
                pool.wait_ge(s_acc, DMA * i)
                nc.gpsimd.indirect_dma_start(out_d, bass.IndirectOffsetOnAxis(ap=ids[:, i:i + 1], axis=0),
                                             y_sb[i % OUT_RING], None, compute_op=ALU.add).then_inc(s_acc, DMA)

            pool.wait_ge(s_ids, 1)
            for n in range(3):
                pool.wait_ge(s_hst[n], DMA * (len(range(n, B, 3)) + (n == 0)))
            first = min(B, IN_RING + OUT_RING)
            pool.wait_ge(s_res[0], (first + 1) * DMA)
            for i in range(IN_RING):
                gather(i)
            pool.wait_ge(s_res[1], (B - first) * DMA)
            for i in range(NT):
                if i and i - 1 + IN_RING < NT:
                    gather(i - 1 + IN_RING)
                add_to_output(i)

        @block.vector
        def _(dve):
            links = [0]

            def link(ins):
                links[0] += 1
                ins.then_inc(s_dve, 1)
                dve.wait_ge(s_dve, links[0])

            def moments(b):
                dve.wait_ge(s_x[b // XCH], DMA)
                link(nc.vector.bn_stats(stats[:, b, :], xs[:, b, :]))
                nc.vector.bn_aggr(mv[:, b, :], stats[:, b, :]).then_inc(s_dve, 1)
                links[0] += 1

            def moments2(b):
                dve.wait_ge(s_x2, b + 1)
                link(nc.vector.bn_stats(stats[:, b, :], xs[:, b, :]))
                nc.vector.bn_aggr(mv2[:, b, :], stats[:, b, :]).then_inc(s_dve, 1)
                links[0] += 1

            def variances(n):
                b0, b1 = chunks[n]
                dve.wait_ge(s_dve, links[0])
                nc.vector.tensor_scalar_add(std[:, b0:b1], mv[:, b0:b1, 1], LN_EPS).then_inc(s_var, 1)

            def inverses(n):
                b0, b1 = chunks[n]
                dve.wait_ge(s_std, n + 1)
                link(nc.vector.reciprocal(rstd[:, b0:b1], std[:, b0:b1]))
                nc.vector.scalar_tensor_tensor(nmr[:, b0:b1], mv[:, b0:b1, 0], -1.0, rstd[:, b0:b1],
                                               ALU.mult, ALU.mult).then_inc(s_rstd, 1)

            def maximum(b, u):
                dve.wait_ge(s_ms, STEPS * b + u + 1)
                if u == 0 and b >= 2:
                    dve.wait_ge(s_mt, 2 * (b - 2) + 2)
                nc.vector.reduce_max(row_max[b % 2][:, u:u + 1], m_ps[(STEPS * b + u) % M_BANKS][:], AX_X).then_inc(s_mx, 1)

            def maxima_rows(b, half):
                n = GROUP * KT
                dve.wait_ge(s_mt, 2 * b + half + 1)
                if b:
                    dve.wait_ge(s_row[half], 2 * DMA * b)
                link(nc.vector.tensor_scalar(m_rows[half][:, 0, :], misc_ps[0:n, 0:P], -1.0, None, ALU.mult))
                nc.vector.scalar_tensor_tensor(m_rows[half][:, 1, :], misc_ps[0:n, 0:P], -1.0, m_rows[half][:, 0, :],
                                               ALU.mult, ALU.subtract).then_inc(s_mr, 1)

            for b in range(*chunks[0]):
                moments(b)
            variances(0)
            inverses(0)
            for v in v_ones:
                nc.vector.memset(v[:, :, :, DH:], 1.0).then_inc(s_ones, 1)
            for k in k_stack:
                nc.vector.memset(k[STACK:SHIFTED, :, :], 1.0).then_inc(s_ones, 1)
            later = list(range(*chunks[1])) if len(chunks) > 1 else []
            dve.wait_ge(s_tanh, 1)
            dve.wait_ge(s_const, n_const * DMA)
            nc.vector.tensor_tensor(tg_bv[:], tgates[:, 0:1], bias[:, 2:3], ALU.mult).then_inc(s_gate, 1)
            for i in TURNS:
                for s in range(STEPS):
                    if is_b(i + 1):
                        maximum(i + 1, s)
                    if s == MAX_AT[1] + 1 and is_b(i):
                        maxima_rows(i, 1)
                    if s == RECIP_AT and is_b(i - 1):
                        dve.wait_ge(s_sc, DMA * i)
                        if i > 1:
                            dve.wait_ge(s_r, DMA * (i - 1))
                        nc.vector.reciprocal(rden_c, den_c).then_inc(s_rc, 1)
                    if s == MAX_AT[0] + 1 and is_b(i + 1):
                        maxima_rows(i + 1, 0)
                    if i >= -1 and s % 2 and later:
                        moments(later.pop(0))
                        if not later:
                            variances(1)
                    if i == 1 and s == 8 and len(chunks) > 1:
                        inverses(1)
                    if s == 10 and is_b(i - 2):
                        moments2(i - 2)

            dve.wait_ge(s_dve, links[0])
            nc.vector.tensor_scalar_add(r2a[:], mv2[:, :, 1], LN_EPS).then_inc(s_var2, 1)
            dve.wait_ge(s_std2, 1)
            link(nc.vector.reciprocal(r2[:], r2a[:]))
            link(nc.vector.tensor_tensor(nmr2[:], mv2[:, :, 1], r2[:], ALU.mult))
            link(nc.vector.tensor_tensor(nmr2[:], nmr2[:], r2[:], ALU.mult))
            nc.vector.tensor_scalar_add(r2a[:], nmr2[:], RMS_EPS).then_inc(s_var2, 1)
            dve.wait_ge(s_std2, 2)
            link(nc.vector.reciprocal(r2a[:], r2a[:]))
            link(nc.vector.tensor_tensor(r2[:], r2[:], r2a[:], ALU.mult))
            link(nc.vector.scalar_tensor_tensor(nmr2[:], mv2[:, :, 0], -1.0, r2[:], ALU.mult, ALU.mult))
            dve.wait_ge(s_pad, 2 * DMA)
            for t in range(B):
                if t >= 3:
                    dve.wait_ge(s_tr, t - 2)
                    n = (t - 3) // 3 + 1 + (t % 3 == 0)
                    dve.wait_ge(s_hst[t % 3], DMA * n)
                link(nc.vector.tensor_scalar(h_in[t % 3], xs[:, t, :], r2[:, t:t + 1], nmr2[:, t:t + 1],
                                             ALU.mult, ALU.add))
                nc.vector.tensor_tensor(h_in[t % 3], h_in[t % 3], w_rms, ALU.mult).then_inc(s_h, 1)

            dve.wait_ge(s_iota, 3)
            for v in (rank, tile_no[:]):
                link(nc.vector.tensor_copy(v, v.bitcast(I32)))
            for k in range(2):
                link(nc.vector.tensor_copy(meta[:, k, :, 0], top[:, 7, :].bitcast(I32)))
            dve.wait_ge(s_setup, 4)
            link(nc.vector.tensor_copy(slot_map[:, :, 0], slot_i[0:NT, :]))
            nc.vector.memset(slot_map[:, :, 1], 0.0).then_inc(s_cc, 1)
            link(nc.vector.memset(restart, 1.0))
            link(nc.vector.memset(by_expert(restart)[:, :, 0:1], 0.0))

            def each(v):
                return v.unsqueeze(2).broadcast_to([P, B, EXPERTS])

            TT = nc.vector.tensor_tensor
            dve.wait_ge(s_lg, B)
            logits = R_PS[:, 0:R].rearrange("p (t e) -> p t e", e=EXPERTS)
            link(nc.vector.reduce_max(top[:, 0, :], logits, AX_X))
            TT(by_token(left), logits, each(top[:, 0, :]), ALU.subtract).then_inc(s_el, 1)
            dve.wait_ge(s_ex, 1)
            link(nc.vector.reduce_sum(top[:, 1, :], by_token(prob), AX_X))
            link(nc.vector.reciprocal(top[:, 1, :], top[:, 1, :]))
            link(TT(by_token(prob), by_token(prob), each(top[:, 1, :]), ALU.mult))

            def choose(k, p):
                link(nc.vector.reduce_max(top[:, 2 + k, :], by_token(p), AX_X))
                link(TT(by_token(r_tmp), by_token(p), each(top[:, 2 + k, :]), ALU.is_equal))
                link(TT(r_tmp, r_tmp, rank, ALU.mult))
                link(nc.vector.reduce_max(top[:, 4, :], by_token(r_tmp), AX_X))
                link(TT(by_token(pick[k]), by_token(rank), each(top[:, 4, :]), ALU.is_equal))

            choose(0, prob)
            link(nc.vector.scalar_tensor_tensor(left, pick[0], -2.0, prob, ALU.mult, ALU.add))
            choose(1, left)
            link(TT(by_expert(chosen[:]).rearrange("p e t -> p t e"), by_token(pick[0]), by_token(pick[1]), ALU.add))
            TT(top[:, 5, :], top[:, 2, :], top[:, 3, :], ALU.add).then_inc(s_ch, 1)
            dve.wait_ge(s_ch, 1)
            link(nc.vector.reciprocal(top[:, 5, :], top[:, 5, :]))
            for k in range(2):
                link(TT(meta[:, k, :, 1], top[:, 2 + k, :], top[:, 5, :], ALU.mult))
            dve.wait_ge(s_cnt, 1)
            in_tile, totals = R_PS[:, 0:R], R_PS[:, R:2 * R]
            link(nc.vector.tensor_tensor_scan(place, restart, totals, 0.0, ALU.mult, ALU.add))
            link(nc.vector.tensor_scalar_add(per_ei[:], by_expert(place)[:, :, B - 1], float(P - 1)))
            shift = P.bit_length() - 1
            link(nc.vector.tensor_single_scalar(per_ei[:], per_ei[:], shift, ALU.arith_shift_right))
            link(nc.vector.tensor_copy(per_e[:, 0, :], per_ei[:]))
            link(nc.vector.memset(per_e[:, 3, :], 1.0))
            link(nc.vector.tensor_tensor_scan(per_e[:, 1, :], per_e[:, 3, :], per_e[:, 0, :], 0.0, ALU.mult, ALU.add))
            link(TT(per_e[:, 2, :], per_e[:, 1, :], per_e[:, 0, :], ALU.subtract))
            link(nc.vector.tensor_scalar(per_e[:, 2, :], per_e[:, 2, :], float(P), None, ALU.mult))
            link(TT(place, place, totals, ALU.subtract))
            link(TT(place, place, in_tile, ALU.add))
            link(TT(by_expert(place), by_expert(place), per_e[:, 2, :].unsqueeze(2).broadcast_to([P, EXPERTS, B]),
                    ALU.add))
            for k in range(2):
                link(TT(by_token(r_tmp), by_token(pick[k]), by_expert(place).rearrange("p e t -> p t e"), ALU.mult))
                link(nc.vector.reduce_sum(top[:, 6, :], by_token(r_tmp), AX_X))
                ins = nc.vector.tensor_copy(slots[:, k, :], top[:, 6, :])
                if k == 0:
                    link(ins)
            ins.then_inc(s_slot, 1)
            le_v = le.rearrange("p (n e) -> p n e", e=EXPERTS)
            link(TT(le_v, per_e[:, 1, :].unsqueeze(1).broadcast_to([P, NT, EXPERTS]),
                    tile_no[:].unsqueeze(2).broadcast_to([P, NT, EXPERTS]), ALU.is_le))
            link(nc.vector.reduce_sum(tile_no[:], le_v, AX_X))
            nc.vector.tensor_scalar(expert_of[:], tile_no[:], float(EXPERTS - 1), None, ALU.min
                                    ).then_inc(s_eid, 1)

            def take_tokens(i):
                dve.wait_ge(s_tr, B + i + 1)
                dve.wait_ge(s_gu, B + i - 2)
                nc.vector.tensor_copy(h_t[(B + i) % 3].rearrange("p c n -> p (c n)"), T_PS[i % 2][:]).then_inc(s_hr, 1)

            def times_up(j):
                dve.wait_ge(s_si, j + 1)
                if j < B:
                    out = act_t[j % 2].rearrange("p c n -> p (c n)")
                    if j >= 2:
                        dve.wait_ge(s_dn, j - 1)
                else:
                    out = act[j % 2]
                    if j >= B + 2:
                        dve.wait_ge(s_ta, j - B - 1)
                nc.vector.tensor_tensor(out, hidden[j % 2], G_PS[j % 2][:, FF:2 * FF], ALU.mult).then_inc(s_a, 1)

            def add_shared(j):
                dve.wait_ge(s_dn, j + 1)
                nc.vector.scalar_tensor_tensor(xs[:, j, :], Y_PS[j % 2][:], tgates[:, 1:2], xs[:, j, :],
                                               ALU.mult, ALU.add).then_inc(s_ysh, 1)

            for j in range(JOBS + 1):
                if B <= j + 1 < JOBS:
                    take_tokens(j + 1 - B)
                if j < JOBS:
                    times_up(j)
                if 1 <= j <= B:
                    add_shared(j - 1)
                if j == TURN_AT:
                    dve.wait_ge(s_mtr, 1)
                    link(nc.vector.tensor_copy(ids[:], R_PS[:, 0:NT]))
                    nc.vector.tensor_scalar(wts[:], R_PS[:, P:P + NT], tgates[:, 1:2], None,
                                            ALU.mult).then_inc(s_ids, 1)

        @block.scalar
        def _(act_e):
            def roots(n):
                b0, b1 = chunks[n]
                act_e.wait_ge(s_var, n + 1)
                nc.scalar.activation(std[:, b0:b1], std[:, b0:b1], ACT.Sqrt).then_inc(s_std, 1)

            roots(0)
            act_e.wait_ge(s_const, n_const * DMA)
            nc.scalar.activation(tgates[:], gates[:], ACT.Tanh).then_inc(s_tanh, 1)

            def evacuate(b, n):
                act_e.wait_ge(s_proj, 3 * b + n + 1)
                if n < 2:
                    if b:
                        act_e.wait_ge(s_part, 6 * (b - 1) + 3 * n + 3)
                    nc.scalar.activation(proj[n], misc_ps[:], ACT.Identity, bias=bias[:, n:n + 1]).then_inc(s_evac, 1)
                    return
                if b >= 3:
                    act_e.wait_ge(s_pv, 8 * (b - 2))
                nc.scalar.copy(v_ones[b % 3][:, :, :, 0:DH],
                               misc_ps[:].rearrange("p (t h d) -> p t h d", t=KT, h=HEADS)).then_inc(s_evac, 1)

            def exponential(b, s):
                n = STEPS * b + s
                act_e.wait_ge(s_es, n + 1)
                group, j = divmod(n, GROUP)
                if j == 0 and group >= 3:
                    act_e.wait_ge(s_pv, group - 2)
                nc.scalar.activation(probs[group % 3][:, j, :], e_ps[n % E_BANKS][:], ACT.Exp,
                                     scale=float(DH) ** -0.5).then_inc(s_exp, 1)

            def take_values(b, g):
                act_e.wait_ge(s_pv, 8 * b + 4 * g + 4)
                if b:
                    act_e.wait_ge(s_w, DMA * b)
                nc.scalar.copy(pv_sb[:, g, :], pv_ps[:]).then_inc(s_u, 1)

            def row(b, half):
                act_e.wait_ge(s_mr, 2 * b + half + 1)
                for n in range(2):
                    act_e.dma_start(q_stack[b % 3][STACK + n:STACK + n + 1, half * GROUP:(half + 1) * GROUP, :],
                                    m_rows[half][:, n, :]).then_inc(s_row[half], DMA)

            for i in TURNS:
                if i == 1 and len(chunks) > 1:
                    roots(1)
                for s in range(STEPS):
                    if is_b(i):
                        exponential(i, s)
                    if s == ROW_AT[1] and is_b(i):
                        row(i, 1)
                    if s == ROW_AT[0] and is_b(i + 1):
                        row(i + 1, 0)
                    if s == VALUES_LATE + 1 and is_b(i - 1):
                        take_values(i - 1, 1)
                    if s == STEPS // 2 + VALUES_LATE + 1 and is_b(i):
                        take_values(i, 0)
                    if s in EVAC_AT and is_b(i + EVAC_AT[s][0]):
                        evacuate(i + EVAC_AT[s][0], EVAC_AT[s][1])

            for n in range(2):
                act_e.wait_ge(s_var2, n + 1)
                nc.scalar.activation(r2a[:], r2a[:], ACT.Sqrt).then_inc(s_std2, 1)

            for t in range(B):
                act_e.wait_ge(s_tr, t + 1)
                if t >= 3:
                    act_e.wait_ge(s_lg, t - 2)
                    act_e.wait_ge(s_hts[t % 3], DMA * (t // 3))
                nc.scalar.copy(h_t[t % 3].rearrange("p c n -> p (c n)"), T_PS[t % 2][:]).then_inc(s_hf, 1)
            act_e.wait_ge(s_el, 1)
            nc.scalar.activation(prob, left, ACT.Exp).then_inc(s_ex, 1)

            def silu(j):
                act_e.wait_ge(s_gu, j + 1)
                if j >= 2:
                    act_e.wait_ge(s_a, j - 1)
                nc.scalar.activation(hidden[j % 2], G_PS[j % 2][:, 0:FF], ACT.Silu).then_inc(s_si, 1)

            def weigh(i):
                j = B + i
                act_e.wait_ge(s_dn, j + 1)
                if i == 0:
                    act_e.wait_ge(s_ids, 1)
                if i == 0:
                    act_e.wait_ge(s_res[0], (min(B, IN_RING + OUT_RING) + 1) * DMA)
                if i >= OUT_RING:
                    act_e.wait_ge(s_acc, DMA * (i - OUT_RING + 1))
                nc.scalar.activation(y_sb[i % OUT_RING], Y_PS[j % 2][:], ACT.Copy, scale=wts[:, i:i + 1]).then_inc(s_yrt, 1)

            def take_act(j):
                act_e.wait_ge(s_ta, j - B + 1)
                act_e.wait_ge(s_dn, j - 1)
                nc.scalar.copy(act_t[j % 2].rearrange("p c n -> p (c n)"), A_PS[:, 0:FF]).then_inc(s_at, 1)

            for j in range(JOBS + 1):
                if j >= B + 1:
                    take_act(j - 1)
                if j < JOBS:
                    silu(j)
                if j >= B + 1:
                    weigh(j - B - 1)

        @block.tensor
        def _(pe):
            def project(b, n):
                if n == 0:
                    pe.wait_ge(s_xn, b + 1)
                    if b == 0:
                        pe.wait_ge(s_const, n_const * DMA)
                    if b >= 2:
                        pe.wait_ge(s_mr, 2 * (b - 2) + 1)
                    elif b == 1:
                        pe.wait_ge(s_evac, 3)
                else:
                    pe.wait_ge(s_evac, 3 * b + n)
                    if n == 2 and b >= 2:
                        pe.wait_ge(s_mr, 2 * (b - 2) + 2)
                if n < 2:
                    nc.tensor.matmul(misc_ps[:], (wq, wk)[n][:], xn[b % 2] if n == 0 else ctx_in[b % 2],
                                     start=True, stop=True).then_inc(s_proj, 1)
                    if n == 0:
                        pe.wait_ge(s_ctx[b % 2], DMA * (b // 2 + 1))
                    return
                for t in range(KT):
                    last = nc.tensor.matmul(misc_ps[:, t * P:(t + 1) * P], ctx_in[b % 2][:, t * P:(t + 1) * P], wv[:],
                                            start=True, stop=True)
                last.then_inc(s_proj, 1)

            def max_scores(b, u):
                h, qt = divmod(u, KT)
                n = STEPS * b + u
                if u == 0:
                    pe.wait_ge(s_rd[b % 3], READS * DMA * (b // 3 + 1))
                if n >= M_BANKS:
                    pe.wait_ge(s_mx, n - M_BANKS + 1)
                nc.tensor.matmul(m_ps[n % M_BANKS][:], q_stack[b % 3][0:STACK, h, qt * P:(qt + 1) * P],
                                 k_stack[b % 3][0:STACK, h, :], start=True, stop=True).then_inc(s_ms, 1)

            def turn_maxima(b, half):
                n = GROUP * KT
                if b == 0 and half == 0:
                    pe.wait_ge(s_setup, 1)
                pe.wait_ge(s_mx, STEPS * b + n * (half + 1))
                if half == 0 and is_b(b + 1):
                    pe.wait_ge(s_evac, 3 * (b + 1) + 3)
                elif half == 1 and is_b(b + 2):
                    pe.wait_ge(s_evac, 3 * (b + 2) + 2)
                else:
                    pe.wait_ge(s_mr, 2 * b + half)
                nc.tensor.transpose(misc_ps[0:n, 0:P], row_max[b % 2][:, n * half:n * (half + 1)],
                                    ident[:]).then_inc(s_mt, 1)

            def exp_scores(b, s):
                g, kt, j = s // (GROUP * KT), s // GROUP % KT, s % GROUP
                h = GROUP * g + j
                n = STEPS * b + s
                if kt == 0 and j == 0:
                    pe.wait_ge(s_row[g], 2 * DMA * (b + 1))
                if n == 0:
                    pe.wait_ge(s_ones, 6)
                if n >= E_BANKS:
                    pe.wait_ge(s_exp, n - E_BANKS + 1)
                nc.tensor.matmul(e_ps[n % E_BANKS][:], k_stack[b % 3][0:SHIFTED, h, kt * P:(kt + 1) * P],
                                 q_stack[b % 3][0:SHIFTED, h, :], start=True, stop=True).then_inc(s_es, 1)

            def values(b, r):
                g, kt = divmod(r, KT)
                pair = 8 * b + r
                pe.wait_ge(s_exp, STEPS * b + GROUP * (r + 1))
                if r == 0:
                    pe.wait_ge(s_evac, 3 * b + 3)
                if kt == 0 and pair:
                    pe.wait_ge(s_u, pair // KT)
                for j in range(GROUP):
                    last = nc.tensor.matmul(pv_ps[2 * DH * j:2 * DH * (j + 1), :], v_ones[b % 3][:, kt, GROUP * g + j, :],
                                            probs[pair % 3][:, j, :], start=(kt == 0), stop=(kt == KT - 1))
                last.then_inc(s_pv, 1)

            for i in TURNS:
                for s in range(STEPS):
                    if is_b(i):
                        exp_scores(i, s)
                    if is_b(i + 1):
                        max_scores(i + 1, s)
                    if s % GROUP == VALUES_LATE:
                        if s < GROUP and is_b(i - 1):
                            values(i - 1, STEPS // GROUP - 1)
                        if s >= GROUP and is_b(i):
                            values(i, s // GROUP - 1)
                    if s == MAX_AT[1] and is_b(i):
                        turn_maxima(i, 1)
                    if s == MAX_AT[0] and is_b(i + 1):
                        turn_maxima(i + 1, 0)
                    if s in PROJECT_AT and is_b(i + PROJECT_AT[s][0]):
                        project(i + PROJECT_AT[s][0], PROJECT_AT[s][1])

            def transpose_tile(src, n):
                for c in range(CHUNKS):
                    last = nc.tensor.transpose(T_PS[n % 2][:, c * P:(c + 1) * P], src[:, c * P:(c + 1) * P], ident[:])
                last.then_inc(s_tr, 1)

            def router_tile(t):
                pe.wait_ge(s_h, t + 1)
                if t >= 2:
                    pe.wait_ge(s_hf, t - 1)
                transpose_tile(h_in[t % 3], t)

            def router_logits(t):
                pe.wait_ge(s_hf, t + 1)
                if t == 0:
                    pe.wait_ge(s_pad, 2 * DMA)
                for c in range(CHUNKS):
                    last = nc.tensor.matmul(R_PS[:, t * EXPERTS:(t + 1) * EXPERTS], h_t[t % 3][:, c, :],
                                            w_router[:, c, :], start=(c == 0), stop=(c == CHUNKS - 1))
                last.then_inc(s_lg, 1)

            router_tile(0)
            for t in range(B):
                if t + 1 < B:
                    router_tile(t + 1)
                router_logits(t)

            def count_choices():
                pe.wait_ge(s_ch, 1)
                pe.wait_ge(s_setup, 4)
                nc.tensor.matmul(R_PS[:, 0:R], before[:], chosen[:], start=True, stop=True)
                nc.tensor.matmul(R_PS[:, R:2 * R], ones[:], chosen[:], start=True, stop=True).then_inc(s_cnt, 1)

            def turn_map():
                pe.wait_ge(s_map, DMA)
                for n in range(2):
                    last = nc.tensor.transpose(R_PS[:, n * P:n * P + NT], slot_map[:, :, n], ident[0:NT, 0:NT])
                last.then_inc(s_mtr, 1)

            def tokens(i):
                pe.wait_ge(s_got[i % IN_RING], DMA * (i // IN_RING + 1))
                if i < 2:
                    pe.wait_ge(s_hf, B - 1 + i)
                else:
                    pe.wait_ge(s_hr, i - 1)
                transpose_tile(gathered[i % IN_RING], i)

            expert = {}

            def routed_weights(j, row):
                return w_routed[:, bass.ds(expert[j], 1), row, :].rearrange("p e n -> p (e n)")

            def gate_up(j):
                if j < B:
                    pe.wait_ge(s_src[j % 3], DMA * (j // 3 + 1))
                    if j == 0:
                        pe.wait_ge(s_wsh, DMA)
                else:
                    pe.wait_ge(s_hr, j - B + 1)
                    if j == B:
                        pe.wait_ge(s_eid, 1)
                        pe.wait_ge(s_wrt, EXPERTS * DMA)
                    expert[j] = pe.value_load(expert_of[0:1, j - B:j - B + 1], min_val=0, max_val=EXPERTS - 1)
                if j >= 2:
                    pe.wait_ge(s_a, j - 1)
                if j < B:
                    for f in range(2 * FF // P):
                        for c in range(CHUNKS):
                            last = nc.tensor.matmul(G_PS[j % 2][:, f * P:(f + 1) * P],
                                                    w_shared[:, c, f * P:(f + 1) * P], h_t[j % 3][:, c, :],
                                                    start=(c == 0), stop=(c == CHUNKS - 1))
                else:
                    for c in range(CHUNKS):
                        last = nc.tensor.matmul(G_PS[j % 2][:], h_t[j % 3][:, c, :], routed_weights(j, c),
                                                start=(c == 0), stop=(c == CHUNKS - 1))
                last.then_inc(s_gu, 1)

            def turn_act(j):
                pe.wait_ge(s_a, j + 1)
                if j > B:
                    pe.wait_ge(s_at, j - B)
                for f in range(FF // P):
                    last = nc.tensor.transpose(A_PS[:, f * P:(f + 1) * P], act[j % 2][:, f * P:(f + 1) * P], ident[:])
                last.then_inc(s_ta, 1)

            def down(j):
                pe.wait_ge(s_a, j + 1) if j < B else pe.wait_ge(s_at, j - B + 1)
                if j >= 2:
                    if j - 2 < B:
                        pe.wait_ge(s_ysh, j - 1)
                    else:
                        pe.wait_ge(s_yrt, j - 1 - B)
                for f in range(FF // P):
                    w = w_shared[:, CHUNKS + f, :] if j < B else routed_weights(j, CHUNKS + f)
                    last = nc.tensor.matmul(Y_PS[j % 2][:], act_t[j % 2][:, f, :], w,
                                            start=(f == 0), stop=(f == FF // P - 1))
                last.then_inc(s_dn, 1)

            count_choices()
            for j in range(JOBS + 1):
                if j == TURN_AT:
                    turn_map()
                if j >= B + 1:
                    turn_act(j - 1)
                if B <= j + 1 < JOBS:
                    tokens(j + 1 - B)
                if j < JOBS:
                    gate_up(j)
                if j >= 1:
                    down(j - 1)


def kernel(**inputs):
    import numpy as np
    from concourse import bacc
    from concourse.bass_utils import run_bass_kernel_spmd

    def attention(name):
        return inputs["L0_xattn_" + name]

    def ffn(name):
        return inputs["L0_ffn_" + name]

    gate = np.concatenate([ffn("sw_gate")[None], ffn("w_gate")])
    up = np.concatenate([ffn("sw_up")[None], ffn("w_up")])
    down = np.concatenate([ffn("sw_down")[None], ffn("w_down")])
    gate_up = np.concatenate([gate, up], axis=2).reshape(EXPERTS + 1, CHUNKS, P, 2 * FF)
    weights = np.concatenate([gate_up, down.reshape(EXPERTS + 1, FF // P, P, L)], axis=1)
    x = inputs["x"]
    arrays = dict(
        x=x, ctx=inputs["ctx_2048"], g_xattn=inputs["g_xattn"].reshape(1, 1), g_ffn=inputs["g_ffn"].reshape(1, 1),
        wq=attention("Wq").T, bq=attention("bq").reshape(P, 1), wk=attention("Wk").T, bk=attention("bk").reshape(P, 1),
        wv=attention("Wv").T, bv=attention("bv").reshape(P, 1), rms=ffn("rms_weight").reshape(1, L),
        router=ffn("router_w"), w=weights.transpose(0, 2, 1, 3))
    arrays = {f"in_{name}": np.ascontiguousarray(value) for name, value in arrays.items()}
    tokens = x.shape[0] * P
    nc = bacc.Bacc("TRN2", target_bir_lowering=False, num_devices=1)
    tensors = [nc.dram_tensor(name, value.shape, mybir.dt.from_np(value.dtype), kind="ExternalInput").ap()
               for name, value in arrays.items()]
    tensors.append(nc.dram_tensor("out", (tokens + P, L), F32, kind="ExternalOutput").ap())
    build(nc, *tensors)
    result = run_bass_kernel_spmd(nc, [arrays], core_ids=[0]).results[0]["out"]
    return result[:tokens].reshape(x.shape)
```

```python
from contextlib import ExitStack

import concourse.bass as bass
from concourse import mybir

F32 = mybir.dt.float32
BF16 = mybir.dt.bfloat16
ALU = mybir.AluOpType
ACT = mybir.ActivationFunctionType
I32 = mybir.dt.int32
AX_X = mybir.AxisListType.X

P = 128
HEADS = 8
DH = P // HEADS
L = 512
KT = L // P
LN_EPS = 1e-5
RMS_EPS = 1e-6
DMA = 16

HI, MID, LO = range(3)
K_PARTS = (HI, MID, LO, HI, MID, HI)
Q_PARTS = (HI, HI, HI, MID, MID, LO)


def runs(parts):
    out = []
    for at, part in enumerate(parts):
        if out and part == out[-1][1] + out[-1][2]:
            out[-1][2] += 1
        else:
            out.append([at, part, 1])
    return out


READS = len(runs(K_PARTS)) + len(runs(Q_PARTS))
STACK = len(K_PARTS) * DH
SHIFTED = STACK + 2

STEPS = HEADS * KT
PROJECT_AT = {21: (3, 0), 24: (3, 1), 7: (2, 2)}
EVAC_AT = {22: (3, 0), 25: (3, 1), 8: (2, 2)}
MAX_AT = (18, 2)
VALUES_LATE = 2
TURN_TOKENS_AT = 10
LOGITS_AT = 13
RECIP_AT = 13
ROW_AT = (24, 9)
GROUP = 4
EXPERTS = 8
FF = 256
CHUNKS = L // P
IN_RING, OUT_RING = 5, 3
ARENA = 34112
W_ROWS = CHUNKS + FF // P
LN_FIRST = 5


class Arena:

    def __init__(self, tensor, start=0):
        self.tensor, self.at = tensor, start

    def take(self, words, dtype=F32):
        view = self.tensor[:, self.at:self.at + words]
        self.at += words
        return view if dtype == F32 else view.bitcast(dtype)


def build(nc, x_d, ctx_d, g_xattn_d, g_ffn_d, wq_d, bq_d, wk_d, bk_d, wv_d, bv_d, rms_d, router_d, w_d, out_d):
    B = x_d.shape[0]
    T = B * P
    NT = 2 * B + EXPERTS - 1
    es = ExitStack()
    with es:
        def sem(name):
            return es.enter_context(nc.semaphore(name))

        def sb(name, shape, dt=F32):
            return es.enter_context(nc.sbuf_tensor(name, shape, dt))

        def psum(name, shape, dt=F32):
            return es.enter_context(nc.psum_tensor(name, shape, dt))

        def dram(name, shape, dt):
            return nc.dram_tensor(name, shape, dt, kind="Internal").ap()

        xs = sb("xs", [P, B, L])
        arena = sb("arena", [P, ARENA])
        a = Arena(arena)
        q_stack = [a.take(HEADS * L // 2, BF16).rearrange("p (h l) -> p h l", h=HEADS) for _ in range(3)]
        k_stack = [a.take(HEADS * L // 2, BF16).rearrange("p (h l) -> p h l", h=HEADS) for _ in range(3)]
        probs = [a.take(GROUP * L).rearrange("p (j l) -> p j l", j=GROUP) for _ in range(3)]
        v_ones = [a.take(KT * HEADS * 2 * DH).rearrange("p (t h e) -> p t h e", t=KT, h=HEADS) for _ in range(3)]
        ctx_in = [a.take(L) for _ in range(2)]
        xn = [a.take(L) for _ in range(2)]
        proj = [a.take(L) for _ in range(2)]
        rest = a.take(L)
        parts = [[a.take(L // 2, BF16) for _ in range(3)] for _ in range(2)]
        wq, wk, wv = (a.take(P) for _ in range(3))
        attention_end = a.at

        a = Arena(arena)
        w_routed = a.take(EXPERTS * W_ROWS * L).rearrange("p (e r n) -> p e r n", e=EXPERTS, r=W_ROWS)
        hidden = [a.take(FF) for _ in range(2)]
        act_t = [a.take(FF).rearrange("p (c n) -> p c n", c=FF // P) for _ in range(2)]
        h_t = [a.take(L).rearrange("p (c n) -> p c n", c=CHUNKS) for _ in range(3)]
        assert a.at >= attention_end, (a.at, attention_end)
        w_rms = a.take(L)
        act = [w_rms[:, n * FF:(n + 1) * FF] for n in range(2)]

        pv_sb = a.take(2 * L).rearrange("p (g l) -> p g l", g=2)
        pv_num = a.take(L)
        pv_rden = a.take(L)
        den_c = a.take(L * HEADS // P)
        rden_c = a.take(L * HEADS // P)
        tok = a.take(L)
        tok_t = a.take(L).rearrange("p (c n) -> p c n", c=CHUNKS)
        logits = a.take(B * EXPERTS)
        w_shared = a.take(W_ROWS * L).rearrange("p (r n) -> p r n", r=W_ROWS)
        assert a.at <= ARENA, a.at
        gathered = [xs[:, n, :] for n in range(IN_RING)]
        y_sb = [xs[:, IN_RING + n, :] for n in range(OUT_RING)]
        R = B * EXPERTS
        a = Arena(w_routed[:, EXPERTS - 1].rearrange("p r n -> p (r n)"))

        def by_token(v):
            return v.rearrange("p (t e) -> p t e", e=EXPERTS)

        def by_expert(v):
            return v.rearrange("p (e t) -> p e t", e=EXPERTS)

        prob = a.take(R)
        left = a.take(R)
        pick = [a.take(R) for _ in range(2)]
        rank = a.take(R)
        r_i = a.take(R, F32)
        r_tmp = a.take(R)
        place = a.take(R)
        restart = a.take(R)
        le = a.take(NT * EXPERTS)

        bias = sb("bias", [P, 3])
        gates = sb("gates", [P, 2])
        tgates = sb("tgates", [P, 2])
        tg_bv = sb("tg_bv", [P, 1])
        ident = sb("ident", [P, P])
        stats = sb("stats", [P, B, 6])
        mv = sb("mv", [P, B, 2])
        std = sb("std", [P, B])
        rstd = sb("rstd", [P, B])
        nmr = sb("nmr", [P, B])
        row_max = [sb(f"row_max{i}", [P, HEADS * KT]) for i in range(2)]
        m_rows = [sb(f"m_rows{i}", [GROUP * KT, 2, P], BF16) for i in range(2)]

        mv2 = sb("mv2", [P, B, 2])
        arg2 = sb("arg2", [P, B])
        half_i = sb("half_i", [P, B], I32)
        r2 = sb("r2", [P, B])
        nmr2 = sb("nmr2", [P, B])
        newton = sb("newton", [P, 1])
        w_router = sb("w_router", [P, CHUNKS, EXPERTS])
        before = sb("before", [P, P], BF16)
        ones = sb("ones", [P, P], BF16)
        top = sb("top", [P, 8, B])
        chosen = sb("chosen", [P, R], BF16)
        slots = sb("slots", [P, 2, B], I32)
        meta = sb("meta", [P, 2, B, 2])
        per_e = sb("per_e", [P, 4, EXPERTS])
        per_ei = sb("per_ei", [P, EXPERTS], I32)
        slot_map = sb("slot_map", [NT, P, 2])
        slot_i = sb("slot_i", [P, P], I32)
        ids = sb("ids", [P, NT], I32)
        wts = sb("wts", [P, NT])
        expert_of = sb("expert_of", [P, NT], I32)
        tile_no = sb("tile_no", [P, NT])

        banks = [psum(f"bank{i}", [P, L]) for i in range(8)]
        E_BANKS, M_BANKS = 3, 3
        e_ps = banks[0:E_BANKS]
        m_ps = banks[E_BANKS:E_BANKS + M_BANKS]
        pv_ps, misc_ps = banks[6:8]

        parts_d = [[dram(f"parts_{n}{i}", (HEADS, 3, DH, L), BF16) for i in range(2)] for n in "qk"]
        pv_d = dram("pv_d", (HEADS, 2 * DH, L), F32)
        rden_d = dram("rden_d", (HEADS, L), F32)
        h_d = dram("h_d", (T + P, L), F32)
        ht_d = dram("ht_d", (B, P, L), F32)
        map_d = dram("map_d", (NT * P, 2), F32)

        s_const = sem("s_const")
        s_setup = sem("s_setup")
        s_ones = sem("s_ones")
        XCH = 4
        s_x = [sem(f"s_xin{i}") for i in range((B + XCH - 1) // XCH)]
        s_ctx = [sem(f"s_ctx{i}") for i in range(2)]
        s_dve = sem("s_dve")
        s_var = sem("s_var")
        s_std = sem("s_std")
        s_rstd = sem("s_rstd")
        s_tanh = sem("s_tanh")
        s_gate = sem("s_gate")
        s_pool = sem("s_pool")
        s_xn = sem("s_xn")
        s_proj = sem("s_proj")
        s_evac = sem("s_evac")
        s_part = sem("s_part")
        s_wr = [sem(f"s_wr{i}") for i in range(2)]
        s_rd = [sem(f"s_rd{i}") for i in range(3)]
        s_ms = sem("s_ms")
        s_mx = sem("s_mx")
        s_mt = sem("s_mt")
        s_mr = sem("s_mr")
        s_row = [sem(f"s_row{i}") for i in range(2)]
        s_es = sem("s_es")
        s_exp = sem("s_exp")
        s_pv = sem("s_pv")
        s_u = sem("s_u")
        s_w = sem("s_w")
        s_sc = sem("s_sc")
        s_rc = sem("s_rc")
        s_r = sem("s_r")
        s_fin = sem("s_fin")
        s_x2 = sem("s_x2")
        s_wsh = sem("s_wsh")
        s_wrt = sem("s_wrt")
        s_guess = sem("s_guess")
        s_h = sem("s_h")
        s_hst = sem("s_hst")
        s_pad = sem("s_pad")
        s_tr = sem("s_tr")
        s_hf = sem("s_hf")
        s_hts = sem("s_hts")
        s_lg = sem("s_lg")
        s_lc = sem("s_lc")
        s_el = sem("s_el")
        s_ex = sem("s_ex")
        s_ch = sem("s_ch")
        s_cnt = sem("s_cnt")
        s_iota = sem("s_iota")
        s_cc = sem("s_cc")
        s_map0 = sem("s_map0")
        s_slot = sem("s_slot")
        s_eid = sem("s_eid")
        s_sc2 = sem("s_sc2")
        s_map = sem("s_map")
        s_mtr = sem("s_mtr")
        s_ids = sem("s_ids")
        s_src = [sem(f"s_src{i}") for i in range(3)]
        s_got = [sem(f"s_got{i}") for i in range(IN_RING)]
        s_hr = sem("s_hr")
        s_gu = sem("s_gu")
        s_si = sem("s_si")
        s_a = sem("s_a")
        s_ta = sem("s_ta")
        s_at = sem("s_at")
        s_dn = sem("s_dn")
        s_ysh = sem("s_ysh")
        s_yrt = sem("s_yrt")
        s_res = [sem(f"s_res{i}") for i in range(2)]
        s_acc = sem("s_acc")

        G_PS = banks[0:2]
        Y_PS = banks[2:4]
        T_PS = banks[4:6]
        A_PS = banks[6]
        R_PS = banks[7]
        JOBS = B + NT
        EXP_AT = 6
        COUNT_AT = 8
        LATE_AT = min(14, B - 3)
        MAP_AT = B - 4
        TURN_AT = B - 3

        chunks = [(0, min(LN_FIRST, B))] + ([(LN_FIRST, B)] if B > LN_FIRST else [])
        n_const = 8
        TURNS = range(-3, B)
        ROUTER_JOBS = {0: B - 3, 3: B - 2, 5: B - 1}

        def is_b(b):
            return 0 <= b < B

        block = es.enter_context(nc.Block())

        @block.sync
        def _(sp):
            def load(dst, src):
                sp.dma_start(dst, src).then_inc(s_const, DMA)

            def load_x(n):
                b0, b1 = n * XCH, min((n + 1) * XCH, B)
                sp.dma_start(xs[:, b0:b1, :], x_d[b0:b1].rearrange("b c l -> c b l")).then_inc(s_x[n], DMA)

            def load_ctx(b):
                if b >= 2:
                    sp.wait_ge(s_proj, 3 * (b - 2) + 3)
                sp.dma_start(ctx_in[b % 2], ctx_d[b]).then_inc(s_ctx[b % 2], DMA)

            load_x(0)
            load(wq[:], wq_d)
            load(wk[:], wk_d)
            load_ctx(0)
            load(wv[:], wv_d)
            load(gates[:, 0:1], g_xattn_d.broadcast_to([P, 1]))
            load(gates[:, 1:2], g_ffn_d.broadcast_to([P, 1]))
            for n, v in enumerate((bq_d, bk_d, bv_d)):
                load(bias[:, n:n + 1], v)
            if B > 1:
                load_ctx(1)
            for n in range(1, len(s_x)):
                load_x(n)

            def write(b, n, part):
                if b >= 2 and part == HI:
                    sp.wait_ge(s_rd[(b - 2) % 3], READS * DMA * ((b - 2) // 3 + 1))
                sp.wait_ge(s_part, 6 * b + 3 * n + part + 1)
                sp.dma_start(parts_d[n][b % 2][:, part, :, :], parts[n][part]).then_inc(s_wr[n], DMA)

            def read(b, n):
                sp.wait_ge(s_wr[n], 3 * DMA * (b + 1))
                if b >= 3 and n == 0:
                    sp.wait_ge(s_es, STEPS * (b - 2))
                src = parts_d[n][b % 2]
                stack = (q_stack, k_stack)[n][b % 3]
                order = (Q_PARTS, K_PARTS)[n]
                for at, part, k in runs(order):
                    sp.dma_start(stack[at * DH:(at + k) * DH, :, :],
                                 src[:, part:part + k].rearrange("h t d l -> (t d) h l")
                                 ).then_inc(s_rd[b % 3], DMA)

            def store_values(b):
                sp.wait_ge(s_u, 2 * b + 2)
                sp.wait_ge(s_fin, 2 * DMA * b)
                sp.dma_start(pv_d.rearrange("(g h) e l -> (h e) g l", g=2), pv_sb).then_inc(s_w, DMA)

            def load_denominators(b):
                sp.wait_ge(s_w, DMA * (b + 1))
                if b:
                    sp.wait_ge(s_rc, b)
                sp.dma_start(den_c, pv_d[:, DH, :].rearrange("h (c w) -> h c w", c=DH)).then_inc(s_sc, DMA)

            def store_reciprocals(b):
                sp.wait_ge(s_rc, b + 1)
                sp.dma_start(rden_d, rden_c).then_inc(s_r, DMA)

            def load_values(b):
                sp.wait_ge(s_r, DMA * (b + 1))
                if b:
                    sp.wait_ge(s_x2, b)
                sp.dma_start(pv_rden, rden_d.unsqueeze(1).broadcast_to([HEADS, DH, L])).then_inc(s_fin, DMA)
                sp.dma_start(pv_num, pv_d[:, 0:DH, :]).then_inc(s_fin, DMA)

            def store_tokens(b):
                sp.wait_ge(s_h, b + 1)
                sp.dma_start(h_d[b * P:(b + 1) * P, :], tok).then_inc(s_hst, DMA)
                if b == 0:
                    sp.dma_start(h_d[T:T + P, :], tok).then_inc(s_hst, DMA)

            def store_turned(b):
                sp.wait_ge(s_hf, b + 1)
                sp.dma_start(ht_d[b], tok_t).then_inc(s_hts, DMA)

            for i in TURNS:
                if is_b(i + 2):
                    read(i + 2, 0)
                if is_b(i - 1):
                    store_values(i - 1)
                if is_b(i + 2):
                    write(i + 2, 1, HI)
                if is_b(i - 1):
                    load_denominators(i - 1)
                if is_b(i + 2):
                    write(i + 2, 1, MID)
                if is_b(i - 1):
                    store_reciprocals(i - 1)
                if is_b(i + 2):
                    write(i + 2, 1, LO)
                if is_b(i + 4) and i + 4 >= 2:
                    load_ctx(i + 4)
                if is_b(i - 3):
                    store_turned(i - 3)
                if is_b(i + 2):
                    read(i + 2, 1)
                if is_b(i - 1):
                    load_values(i - 1)
                if is_b(i - 2):
                    store_tokens(i - 2)
                if is_b(i + 3):
                    for part in (HI, MID, LO):
                        write(i + 3, 0, part)
                if i == 0:
                    sp.dma_start(w_router[:], router_d.rearrange("(c p) e -> p c e", p=P)).then_inc(s_pad, DMA)
                    sp.dma_start(w_rms, rms_d.broadcast_to([P, L])).then_inc(s_pad, DMA)
                    sp.dma_start(w_shared, w_d[0]).then_inc(s_wsh, DMA)

            def load_expert(e):
                sp.dma_start(w_routed[:, e], w_d[1 + e]).then_inc(s_wrt, DMA)

            def source(j):
                sp.wait_ge(s_hts, DMA * (j + 1))
                if j >= 3:
                    sp.wait_ge(s_gu, j - 2)
                sp.dma_start(h_t[j % 3], ht_d[j]).then_inc(s_src[j % 3], DMA)

            for j in range(B + 3):
                if j < B:
                    source(j)
                if j == 2:
                    store_values(B - 1)
                    store_turned(B - 3)
                    load_denominators(B - 1)
                if j == 3:
                    store_reciprocals(B - 1)
                if j >= 3:
                    sp.wait_ge(s_ysh, j - 2)
                    sp.dma_start(out_d[(j - 3) * P:(j - 2) * P, :], xs[:, j - 3, :]
                                 ).then_inc(s_res[j - 3 >= IN_RING + OUT_RING], DMA)
                if j == 3:
                    sp.dma_start(out_d[T:T + P, :], xs[:, 0, :]).then_inc(s_res[0], DMA)
                    store_tokens(B - 2)
                    load_values(B - 1)
                if j == 6:
                    store_turned(B - 2)
                    sp.wait_ge(s_cc, 1)
                    sp.dma_start(map_d.rearrange("(n s) k -> n s k", s=P), slot_map[:]).then_inc(s_map0, DMA)
                if j == 7:
                    store_tokens(B - 1)
                if j == 8:
                    store_turned(B - 1)
                if 5 <= j < 5 + EXPERTS - 1:
                    load_expert(j - 5)
                if j == LATE_AT:
                    sp.wait_ge(s_eid, 1)
                    load_expert(EXPERTS - 1)
                if j == MAP_AT:
                    sp.wait_ge(s_sc2, 2 * B * DMA)
                    sp.dma_start(slot_map[:], map_d.rearrange("(n s) k -> n s k", s=P)).then_inc(s_map, DMA)
            sp.wait_ge(s_acc, NT * DMA)

        @block.gpsimd
        def _(pool):
            links = [0]

            def link(ins):
                links[0] += 1
                ins.then_inc(s_pool, 1)
                pool.wait_ge(s_pool, links[0])

            link(nc.gpsimd.memset(ident[:], 0.0))
            nc.gpsimd.affine_select(out=ident[:], in_=ident[:], compare_op=ALU.not_equal, fill=1.0, base=0,
                                    pattern=[[-1, P]], channel_multiplier=1).then_inc(s_setup, 1)

            def normalise(b):
                pool.wait_ge(s_rstd, 1 if b < LN_FIRST else 2)
                if b >= 2:
                    pool.wait_ge(s_proj, 3 * (b - 2) + 2)
                nc.gpsimd.tensor_scalar(xn[b % 2], xs[:, b, :], rstd[:, b:b + 1], nmr[:, b:b + 1],
                                        ALU.mult, ALU.add).then_inc(s_xn, 1)

            def split(b, n):
                pool.wait_ge(s_evac, 3 * b + n + 1)
                if b:
                    pool.wait_ge(s_wr[n], 3 * DMA * b)
                hi, mid, lo = parts[n]

                def both(ins):
                    ins.then_inc(s_part, 1)
                    return ins

                both(nc.gpsimd.tensor_scalar(hi, proj[n], 1.0, None, ALU.mult))
                pool.wait_ge(s_part, 6 * b + 3 * n + 1)
                link(nc.gpsimd.tensor_tensor(rest, proj[n], hi, ALU.subtract))
                both(nc.gpsimd.tensor_scalar(mid, rest, 1.0, None, ALU.mult))
                pool.wait_ge(s_part, 6 * b + 3 * n + 2)
                both(nc.gpsimd.tensor_tensor(lo, rest, mid, ALU.subtract))
                pool.wait_ge(s_part, 6 * b + 3 * n + 3)

            def add_attention(b):
                pool.wait_ge(s_fin, 2 * DMA * (b + 1))
                if b == 0:
                    pool.wait_ge(s_gate, 1)
                link(nc.gpsimd.tensor_tensor(pv_num, pv_num, pv_rden, ALU.mult))
                link(nc.gpsimd.tensor_scalar(pv_num, pv_num, tgates[:, 0:1], tg_bv[:], ALU.mult, ALU.add))
                nc.gpsimd.tensor_tensor(xs[:, b, :], xs[:, b, :], pv_num, ALU.add).then_inc(s_x2, 1)
                pool.wait_ge(s_x2, b + 1)

            link(nc.gpsimd.memset(before[:], 1.0))
            nc.gpsimd.affine_select(out=before[:], in_=before[:], compare_op=ALU.is_gt, fill=0.0, base=0,
                                    pattern=[[1, P]], channel_multiplier=-1).then_inc(s_setup, 1)
            nc.gpsimd.memset(ones[:], 1.0).then_inc(s_setup, 1)
            nc.gpsimd.iota(slot_i[:], pattern=[[1, P]], base=T, channel_multiplier=0).then_inc(s_setup, 1)

            def tokens(b):
                pool.wait_ge(s_guess, b + 1)
                r, arg = r2[:, b:b + 1], arg2[:, b:b + 1]
                for _ in range(3):
                    link(nc.gpsimd.tensor_scalar(newton[:], r, r, arg, ALU.mult, ALU.mult))
                    link(nc.gpsimd.tensor_scalar(newton[:], newton[:], -0.5, 1.5, ALU.mult, ALU.add))
                    link(nc.gpsimd.tensor_tensor(r, r, newton[:], ALU.mult))
                link(nc.gpsimd.tensor_scalar(nmr2[:, b:b + 1], mv2[:, b, 0:1], r, -1.0, ALU.mult, ALU.mult))
                if b:
                    pool.wait_ge(s_tr, b)
                    pool.wait_ge(s_hst, DMA * (b + 1))
                else:
                    pool.wait_ge(s_pad, 2 * DMA)
                link(nc.gpsimd.tensor_scalar(tok, xs[:, b, :], r, nmr2[:, b:b + 1], ALU.mult, ALU.add))
                nc.gpsimd.tensor_tensor(tok, tok, w_rms, ALU.mult).then_inc(s_h, 1)
                pool.wait_ge(s_h, b + 1)

            normalise(0)
            for i in TURNS:
                if is_b(i + 2):
                    split(i + 2, 1)
                if is_b(i + 4):
                    normalise(i + 4)
                if is_b(i - 2):
                    tokens(i - 2)
                if is_b(i + 3):
                    split(i + 3, 0)
                if is_b(i - 1):
                    add_attention(i - 1)
            tokens(B - 2)
            add_attention(B - 1)
            tokens(B - 1)

            for out, pattern, base, cm in (
                    (by_token(rank), [[0, B], [-1, EXPERTS]], EXPERTS, 0),
                    (tile_no[:], [[1, NT]], 0, 0),
                    (top[:, 7, :], [[P, B]], 0, 1)):
                nc.gpsimd.iota(out.bitcast(I32), pattern=pattern, base=base, channel_multiplier=cm).then_inc(s_iota, 1)

            pool.wait_ge(s_slot, 1)
            pool.wait_ge(s_map0, DMA)
            for k in range(2):
                for t in range(B):
                    nc.gpsimd.indirect_dma_start(
                        map_d, bass.IndirectOffsetOnAxis(ap=slots[:, k, t:t + 1], axis=0),
                        meta[:, k, t, :], None).then_inc(s_sc2, DMA)
            def gather(i):
                if i >= IN_RING:
                    pool.wait_ge(s_tr, B + i - IN_RING + 1)
                nc.gpsimd.indirect_dma_start(gathered[i % IN_RING], None, h_d,
                                             bass.IndirectOffsetOnAxis(ap=ids[:, i:i + 1], axis=0)
                                             ).then_inc(s_got[i % IN_RING], DMA)

            def add_to_output(i):
                pool.wait_ge(s_yrt, i + 1)
                pool.wait_ge(s_acc, DMA * i)
                nc.gpsimd.indirect_dma_start(out_d, bass.IndirectOffsetOnAxis(ap=ids[:, i:i + 1], axis=0),
                                             y_sb[i % OUT_RING], None, compute_op=ALU.add).then_inc(s_acc, DMA)

            pool.wait_ge(s_ids, 1)
            pool.wait_ge(s_hst, DMA * (B + 1))
            first = min(B, IN_RING + OUT_RING)
            pool.wait_ge(s_res[0], (first + 1) * DMA)
            for i in range(IN_RING):
                gather(i)
            pool.wait_ge(s_res[1], (B - first) * DMA)
            for i in range(NT):
                if i and i - 1 + IN_RING < NT:
                    gather(i - 1 + IN_RING)
                add_to_output(i)

        @block.vector
        def _(dve):
            links = [0]

            def link(ins):
                links[0] += 1
                ins.then_inc(s_dve, 1)
                dve.wait_ge(s_dve, links[0])

            def moments(b):
                dve.wait_ge(s_x[b // XCH], DMA)
                link(nc.vector.bn_stats(stats[:, b, :], xs[:, b, :]))
                nc.vector.bn_aggr(mv[:, b, :], stats[:, b, :]).then_inc(s_dve, 1)
                links[0] += 1

            def moments2(b):
                dve.wait_ge(s_x2, b + 1)
                arg, half = arg2[:, b:b + 1], half_i[:, b:b + 1]
                link(nc.vector.bn_stats(stats[:, b, :], xs[:, b, :]))
                link(nc.vector.bn_aggr(mv2[:, b, :], stats[:, b, :]))
                link(nc.vector.tensor_scalar(arg, mv2[:, b, 1:2], 1.0 + RMS_EPS, LN_EPS * RMS_EPS, ALU.mult, ALU.add))
                link(nc.vector.tensor_single_scalar(half, arg.bitcast(I32), 1, ALU.arith_shift_right))
                nc.vector.tensor_scalar(r2[:, b:b + 1].bitcast(I32), half, -1.0, float(0x5F3759DF), ALU.mult, ALU.add
                                        ).then_inc(s_guess, 1)

            def take_logits(b):
                dve.wait_ge(s_lg, b + 1)
                nc.vector.tensor_copy(logits[:, b * EXPERTS:(b + 1) * EXPERTS], misc_ps[:, 0:EXPERTS]
                                      ).then_inc(s_lc, 1)

            def invert(b):
                dve.wait_ge(s_sc, DMA * (b + 1))
                if b:
                    dve.wait_ge(s_r, DMA * b)
                nc.vector.reciprocal(rden_c, den_c).then_inc(s_rc, 1)

            def variances(n):
                b0, b1 = chunks[n]
                dve.wait_ge(s_dve, links[0])
                nc.vector.tensor_scalar_add(std[:, b0:b1], mv[:, b0:b1, 1], LN_EPS).then_inc(s_var, 1)

            def inverses(n):
                b0, b1 = chunks[n]
                dve.wait_ge(s_std, n + 1)
                link(nc.vector.reciprocal(rstd[:, b0:b1], std[:, b0:b1]))
                nc.vector.scalar_tensor_tensor(nmr[:, b0:b1], mv[:, b0:b1, 0], -1.0, rstd[:, b0:b1],
                                               ALU.mult, ALU.mult).then_inc(s_rstd, 1)

            def maximum(b, u):
                dve.wait_ge(s_ms, STEPS * b + u + 1)
                if u == 0 and b >= 2:
                    dve.wait_ge(s_mt, 2 * (b - 2) + 2)
                nc.vector.reduce_max(row_max[b % 2][:, u:u + 1], m_ps[(STEPS * b + u) % M_BANKS][:], AX_X).then_inc(s_mx, 1)

            def maxima_rows(b, half):
                n = GROUP * KT
                dve.wait_ge(s_mt, 2 * b + half + 1)
                if b:
                    dve.wait_ge(s_row[half], 2 * DMA * b)
                link(nc.vector.tensor_scalar(m_rows[half][:, 0, :], misc_ps[0:n, 0:P], -1.0, None, ALU.mult))
                nc.vector.scalar_tensor_tensor(m_rows[half][:, 1, :], misc_ps[0:n, 0:P], -1.0, m_rows[half][:, 0, :],
                                               ALU.mult, ALU.subtract).then_inc(s_mr, 1)

            for b in range(*chunks[0]):
                moments(b)
            variances(0)
            inverses(0)
            for v in v_ones:
                nc.vector.memset(v[:, :, :, DH:], 1.0).then_inc(s_ones, 1)
            for k in k_stack:
                nc.vector.memset(k[STACK:SHIFTED, :, :], 1.0).then_inc(s_ones, 1)
            later = list(range(*chunks[1])) if len(chunks) > 1 else []
            dve.wait_ge(s_tanh, 1)
            dve.wait_ge(s_const, n_const * DMA)
            nc.vector.tensor_tensor(tg_bv[:], tgates[:, 0:1], bias[:, 2:3], ALU.mult).then_inc(s_gate, 1)
            for i in TURNS:
                for s in range(STEPS):
                    if is_b(i + 1):
                        maximum(i + 1, s)
                    if s == MAX_AT[1] + 1 and is_b(i):
                        maxima_rows(i, 1)
                    if s == RECIP_AT and is_b(i - 1):
                        invert(i - 1)
                    if s == MAX_AT[0] + 1 and is_b(i + 1):
                        maxima_rows(i + 1, 0)
                    if i >= -1 and s % 2 and later:
                        moments(later.pop(0))
                        if not later:
                            variances(1)
                    if i == 1 and s == 8 and len(chunks) > 1:
                        inverses(1)
                    if s == 10 and is_b(i - 2):
                        moments2(i - 2)
                    if s == LOGITS_AT + 1 and is_b(i - 3):
                        take_logits(i - 3)

            TT = nc.vector.tensor_tensor

            def each(v):
                return v.unsqueeze(2).broadcast_to([P, B, EXPERTS])

            def routing():
                dve.wait_ge(s_iota, 3)
                for v in (rank, tile_no[:]):
                    link(nc.vector.tensor_copy(v, v.bitcast(I32)))
                for k in range(2):
                    link(nc.vector.tensor_copy(meta[:, k, :, 0], top[:, 7, :].bitcast(I32)))
                dve.wait_ge(s_setup, 4)
                link(nc.vector.tensor_copy(slot_map[:, :, 0], slot_i[0:NT, :]))
                nc.vector.memset(slot_map[:, :, 1], 0.0).then_inc(s_cc, 1)
                link(nc.vector.memset(restart, 1.0))
                link(nc.vector.memset(by_expert(restart)[:, :, 0:1], 0.0))

                yield
                logits_t = by_token(logits)
                dve.wait_ge(s_lc, B)
                link(nc.vector.reduce_max(top[:, 0, :], logits_t, AX_X))
                TT(by_token(left), logits_t, each(top[:, 0, :]), ALU.subtract).then_inc(s_el, 1)
                yield
                dve.wait_ge(s_ex, 1)
                link(nc.vector.reduce_sum(top[:, 1, :], by_token(prob), AX_X))
                link(nc.vector.reciprocal(top[:, 1, :], top[:, 1, :]))
                link(TT(by_token(prob), by_token(prob), each(top[:, 1, :]), ALU.mult))

                def choose(k, p):
                    link(nc.vector.reduce_max(top[:, 2 + k, :], by_token(p), AX_X))
                    link(TT(by_token(r_tmp), by_token(p), each(top[:, 2 + k, :]), ALU.is_equal))
                    link(TT(r_tmp, r_tmp, rank, ALU.mult))
                    link(nc.vector.reduce_max(top[:, 4, :], by_token(r_tmp), AX_X))
                    link(TT(by_token(pick[k]), by_token(rank), each(top[:, 4, :]), ALU.is_equal))

                choose(0, prob)
                link(nc.vector.scalar_tensor_tensor(left, pick[0], -2.0, prob, ALU.mult, ALU.add))
                yield
                choose(1, left)
                link(TT(by_expert(chosen[:]).rearrange("p e t -> p t e"), by_token(pick[0]), by_token(pick[1]), ALU.add))
                TT(top[:, 5, :], top[:, 2, :], top[:, 3, :], ALU.add).then_inc(s_ch, 1)
                yield
                dve.wait_ge(s_ch, 1)
                link(nc.vector.reciprocal(top[:, 5, :], top[:, 5, :]))
                for k in range(2):
                    link(TT(meta[:, k, :, 1], top[:, 2 + k, :], top[:, 5, :], ALU.mult))
                dve.wait_ge(s_cnt, 1)
                in_tile, totals = R_PS[:, 0:R], R_PS[:, R:2 * R]
                link(nc.vector.tensor_tensor_scan(place, restart, totals, 0.0, ALU.mult, ALU.add))
                link(nc.vector.tensor_scalar_add(per_ei[:], by_expert(place)[:, :, B - 1], float(P - 1)))
                shift = P.bit_length() - 1
                link(nc.vector.tensor_single_scalar(per_ei[:], per_ei[:], shift, ALU.arith_shift_right))
                link(nc.vector.tensor_copy(per_e[:, 0, :], per_ei[:]))
                link(nc.vector.memset(per_e[:, 3, :], 1.0))
                link(nc.vector.tensor_tensor_scan(per_e[:, 1, :], per_e[:, 3, :], per_e[:, 0, :], 0.0, ALU.mult, ALU.add))
                link(TT(per_e[:, 2, :], per_e[:, 1, :], per_e[:, 0, :], ALU.subtract))
                link(nc.vector.tensor_scalar(per_e[:, 2, :], per_e[:, 2, :], float(P), None, ALU.mult))
                yield
                link(TT(place, place, totals, ALU.subtract))
                link(TT(place, place, in_tile, ALU.add))
                link(TT(by_expert(place), by_expert(place), per_e[:, 2, :].unsqueeze(2).broadcast_to([P, EXPERTS, B]),
                        ALU.add))
                for k in range(2):
                    link(TT(by_token(r_tmp), by_token(pick[k]), by_expert(place).rearrange("p e t -> p t e"), ALU.mult))
                    link(nc.vector.reduce_sum(top[:, 6, :], by_token(r_tmp), AX_X))
                    ins = nc.vector.tensor_copy(slots[:, k, :], top[:, 6, :])
                    if k == 0:
                        link(ins)
                        yield
                ins.then_inc(s_slot, 1)
                yield
                le_v = le.rearrange("p (n e) -> p n e", e=EXPERTS)
                link(TT(le_v, per_e[:, 1, :].unsqueeze(1).broadcast_to([P, NT, EXPERTS]),
                        tile_no[:].unsqueeze(2).broadcast_to([P, NT, EXPERTS]), ALU.is_le))
                link(nc.vector.reduce_sum(tile_no[:], le_v, AX_X))
                nc.vector.tensor_scalar(expert_of[:], tile_no[:], float(EXPERTS - 1), None, ALU.min
                                        ).then_inc(s_eid, 1)

            def take_tokens(i):
                dve.wait_ge(s_tr, B + i + 1)
                dve.wait_ge(s_gu, B + i - 2)
                nc.vector.tensor_copy(h_t[(B + i) % 3].rearrange("p c n -> p (c n)"), T_PS[i % 2][:]).then_inc(s_hr, 1)

            def times_up(j):
                dve.wait_ge(s_si, j + 1)
                if j < B:
                    out = act_t[j % 2].rearrange("p c n -> p (c n)")
                    if j >= 2:
                        dve.wait_ge(s_dn, j - 1)
                else:
                    out = act[j % 2]
                    if j >= B + 2:
                        dve.wait_ge(s_ta, j - B - 1)
                nc.vector.tensor_tensor(out, hidden[j % 2], G_PS[j % 2][:, FF:2 * FF], ALU.mult).then_inc(s_a, 1)

            def add_shared(j):
                dve.wait_ge(s_dn, j + 1)
                nc.vector.scalar_tensor_tensor(xs[:, j, :], Y_PS[j % 2][:], tgates[:, 1:2], xs[:, j, :],
                                               ALU.mult, ALU.add).then_inc(s_ysh, 1)

            pieces = routing()
            for j in range(JOBS + 1):
                if j == 1:
                    invert(B - 1)
                if j == 3:
                    moments2(B - 1)
                if B <= j + 1 < JOBS:
                    take_tokens(j + 1 - B)
                if j < JOBS:
                    times_up(j)
                if j == 0:
                    moments2(B - 2)
                if j in ROUTER_JOBS:
                    take_logits(ROUTER_JOBS[j])
                if 1 <= j <= B:
                    add_shared(j - 1)
                if j >= 4:
                    next(pieces, None)
                if j == TURN_AT:
                    dve.wait_ge(s_mtr, 1)
                    link(nc.vector.tensor_copy(ids[:], R_PS[:, 0:NT]))
                    nc.vector.tensor_scalar(wts[:], R_PS[:, P:P + NT], tgates[:, 1:2], None,
                                            ALU.mult).then_inc(s_ids, 1)

        @block.scalar
        def _(act_e):
            def roots(n):
                b0, b1 = chunks[n]
                act_e.wait_ge(s_var, n + 1)
                nc.scalar.activation(std[:, b0:b1], std[:, b0:b1], ACT.Sqrt).then_inc(s_std, 1)

            roots(0)
            act_e.wait_ge(s_const, n_const * DMA)
            nc.scalar.activation(tgates[:], gates[:], ACT.Tanh).then_inc(s_tanh, 1)

            def evacuate(b, n):
                act_e.wait_ge(s_proj, 3 * b + n + 1)
                if n < 2:
                    if b:
                        act_e.wait_ge(s_part, 6 * (b - 1) + 3 * n + 3)
                    nc.scalar.activation(proj[n], misc_ps[:], ACT.Identity, bias=bias[:, n:n + 1]).then_inc(s_evac, 1)
                    return
                if b >= 3:
                    act_e.wait_ge(s_pv, 8 * (b - 2))
                nc.scalar.copy(v_ones[b % 3][:, :, :, 0:DH],
                               misc_ps[:].rearrange("p (t h d) -> p t h d", t=KT, h=HEADS)).then_inc(s_evac, 1)

            def exponential(b, s):
                n = STEPS * b + s
                act_e.wait_ge(s_es, n + 1)
                group, j = divmod(n, GROUP)
                if j == 0 and group >= 3:
                    act_e.wait_ge(s_pv, group - 2)
                nc.scalar.activation(probs[group % 3][:, j, :], e_ps[n % E_BANKS][:], ACT.Exp,
                                     scale=float(DH) ** -0.5).then_inc(s_exp, 1)

            def take_values(b, g):
                act_e.wait_ge(s_pv, 8 * b + 4 * g + 4)
                if b:
                    act_e.wait_ge(s_w, DMA * b)
                nc.scalar.copy(pv_sb[:, g, :], pv_ps[:]).then_inc(s_u, 1)

            def take_turned(b):
                act_e.wait_ge(s_tr, b + 1)
                if b:
                    act_e.wait_ge(s_lg, b)
                    act_e.wait_ge(s_hts, DMA * b)
                nc.scalar.copy(tok_t.rearrange("p c n -> p (c n)"), misc_ps[:]).then_inc(s_hf, 1)

            def row(b, half):
                act_e.wait_ge(s_mr, 2 * b + half + 1)
                for n in range(2):
                    act_e.dma_start(q_stack[b % 3][STACK + n:STACK + n + 1, half * GROUP:(half + 1) * GROUP, :],
                                    m_rows[half][:, n, :]).then_inc(s_row[half], DMA)

            for i in TURNS:
                if i == 1 and len(chunks) > 1:
                    roots(1)
                for s in range(STEPS):
                    if is_b(i):
                        exponential(i, s)
                    if s == ROW_AT[1] and is_b(i):
                        row(i, 1)
                    if s == ROW_AT[0] and is_b(i + 1):
                        row(i + 1, 0)
                    if s == TURN_TOKENS_AT + 1 and is_b(i - 3):
                        take_turned(i - 3)
                    if s == VALUES_LATE + 1 and is_b(i - 1):
                        take_values(i - 1, 1)
                    if s == STEPS // 2 + VALUES_LATE + 1 and is_b(i):
                        take_values(i, 0)
                    if s in EVAC_AT and is_b(i + EVAC_AT[s][0]):
                        evacuate(i + EVAC_AT[s][0], EVAC_AT[s][1])

            take_values(B - 1, 1)

            def silu(j):
                act_e.wait_ge(s_gu, j + 1)
                if j >= 2:
                    act_e.wait_ge(s_a, j - 1)
                nc.scalar.activation(hidden[j % 2], G_PS[j % 2][:, 0:FF], ACT.Silu).then_inc(s_si, 1)

            def weigh(i):
                j = B + i
                act_e.wait_ge(s_dn, j + 1)
                if i == 0:
                    act_e.wait_ge(s_ids, 1)
                if i == 0:
                    act_e.wait_ge(s_res[0], (min(B, IN_RING + OUT_RING) + 1) * DMA)
                if i >= OUT_RING:
                    act_e.wait_ge(s_acc, DMA * (i - OUT_RING + 1))
                nc.scalar.activation(y_sb[i % OUT_RING], Y_PS[j % 2][:], ACT.Copy, scale=wts[:, i:i + 1]).then_inc(s_yrt, 1)

            def take_act(j):
                act_e.wait_ge(s_ta, j - B + 1)
                act_e.wait_ge(s_dn, j - 1)
                nc.scalar.copy(act_t[j % 2].rearrange("p c n -> p (c n)"), A_PS[:, 0:FF]).then_inc(s_at, 1)

            for j in range(JOBS + 1):
                if j in ROUTER_JOBS:
                    take_turned(ROUTER_JOBS[j])
                if j == EXP_AT:
                    act_e.wait_ge(s_el, 1)
                    nc.scalar.activation(prob, left, ACT.Exp).then_inc(s_ex, 1)
                if j >= B + 1:
                    take_act(j - 1)
                if j < JOBS:
                    silu(j)
                if j >= B + 1:
                    weigh(j - B - 1)

        @block.tensor
        def _(pe):
            misc_reader = [None]

            def take_misc(reader, count):
                if misc_reader[0]:
                    pe.wait_ge(*misc_reader[0])
                misc_reader[0] = (reader, count)

            def project(b, n):
                take_misc(s_evac, 3 * b + n + 1)
                if n == 0:
                    pe.wait_ge(s_xn, b + 1)
                    if b == 0:
                        pe.wait_ge(s_const, n_const * DMA)
                if n < 2:
                    nc.tensor.matmul(misc_ps[:], (wq, wk)[n][:], xn[b % 2] if n == 0 else ctx_in[b % 2],
                                     start=True, stop=True).then_inc(s_proj, 1)
                    if n == 0:
                        pe.wait_ge(s_ctx[b % 2], DMA * (b // 2 + 1))
                    return
                for t in range(KT):
                    last = nc.tensor.matmul(misc_ps[:, t * P:(t + 1) * P], ctx_in[b % 2][:, t * P:(t + 1) * P], wv[:],
                                            start=True, stop=True)
                last.then_inc(s_proj, 1)

            def max_scores(b, u):
                h, qt = divmod(u, KT)
                n = STEPS * b + u
                if u == 0:
                    pe.wait_ge(s_rd[b % 3], READS * DMA * (b // 3 + 1))
                if n >= M_BANKS:
                    pe.wait_ge(s_mx, n - M_BANKS + 1)
                nc.tensor.matmul(m_ps[n % M_BANKS][:], q_stack[b % 3][0:STACK, h, qt * P:(qt + 1) * P],
                                 k_stack[b % 3][0:STACK, h, :], start=True, stop=True).then_inc(s_ms, 1)

            def turn_maxima(b, half):
                n = GROUP * KT
                if b == 0 and half == 0:
                    pe.wait_ge(s_setup, 1)
                pe.wait_ge(s_mx, STEPS * b + n * (half + 1))
                take_misc(s_mr, 2 * b + half + 1)
                nc.tensor.transpose(misc_ps[0:n, 0:P], row_max[b % 2][:, n * half:n * (half + 1)],
                                    ident[:]).then_inc(s_mt, 1)

            def exp_scores(b, s):
                g, kt, j = s // (GROUP * KT), s // GROUP % KT, s % GROUP
                h = GROUP * g + j
                n = STEPS * b + s
                if kt == 0 and j == 0:
                    pe.wait_ge(s_row[g], 2 * DMA * (b + 1))
                if n == 0:
                    pe.wait_ge(s_ones, 6)
                if n >= E_BANKS:
                    pe.wait_ge(s_exp, n - E_BANKS + 1)
                nc.tensor.matmul(e_ps[n % E_BANKS][:], k_stack[b % 3][0:SHIFTED, h, kt * P:(kt + 1) * P],
                                 q_stack[b % 3][0:SHIFTED, h, :], start=True, stop=True).then_inc(s_es, 1)

            def transpose_tile(out, src):
                for c in range(CHUNKS):
                    last = nc.tensor.transpose(out[:, c * P:(c + 1) * P], src[:, c * P:(c + 1) * P], ident[:])
                last.then_inc(s_tr, 1)

            def turn_tokens(b):
                take_misc(s_hf, b + 1)
                pe.wait_ge(s_h, b + 1)
                transpose_tile(misc_ps, tok)

            def router_logits(b):
                take_misc(s_lc, b + 1)
                for c in range(CHUNKS):
                    last = nc.tensor.matmul(misc_ps[:, 0:EXPERTS], tok_t[:, c, :], w_router[:, c, :],
                                            start=(c == 0), stop=(c == CHUNKS - 1))
                last.then_inc(s_lg, 1)

            def values(b, r):
                g, kt = divmod(r, KT)
                pair = 8 * b + r
                pe.wait_ge(s_exp, STEPS * b + GROUP * (r + 1))
                if r == 0:
                    pe.wait_ge(s_evac, 3 * b + 3)
                if kt == 0 and pair:
                    pe.wait_ge(s_u, pair // KT)
                for j in range(GROUP):
                    last = nc.tensor.matmul(pv_ps[2 * DH * j:2 * DH * (j + 1), :], v_ones[b % 3][:, kt, GROUP * g + j, :],
                                            probs[pair % 3][:, j, :], start=(kt == 0), stop=(kt == KT - 1))
                last.then_inc(s_pv, 1)

            for i in TURNS:
                for s in range(STEPS):
                    if is_b(i):
                        exp_scores(i, s)
                    if is_b(i + 1):
                        max_scores(i + 1, s)
                    if s % GROUP == VALUES_LATE:
                        if s < GROUP and is_b(i - 1):
                            values(i - 1, STEPS // GROUP - 1)
                        if s >= GROUP and is_b(i):
                            values(i, s // GROUP - 1)
                    if s == MAX_AT[1] and is_b(i):
                        turn_maxima(i, 1)
                    if s == MAX_AT[0] and is_b(i + 1):
                        turn_maxima(i + 1, 0)
                    if s == TURN_TOKENS_AT and is_b(i - 3):
                        turn_tokens(i - 3)
                    if s == LOGITS_AT and is_b(i - 3):
                        router_logits(i - 3)
                    if s in PROJECT_AT and is_b(i + PROJECT_AT[s][0]):
                        project(i + PROJECT_AT[s][0], PROJECT_AT[s][1])

            values(B - 1, STEPS // GROUP - 1)

            def count_choices():
                pe.wait_ge(s_ch, 1)
                pe.wait_ge(s_setup, 4)
                nc.tensor.matmul(R_PS[:, 0:R], before[:], chosen[:], start=True, stop=True)
                nc.tensor.matmul(R_PS[:, R:2 * R], ones[:], chosen[:], start=True, stop=True).then_inc(s_cnt, 1)

            def turn_map():
                pe.wait_ge(s_map, DMA)
                for n in range(2):
                    last = nc.tensor.transpose(R_PS[:, n * P:n * P + NT], slot_map[:, :, n], ident[0:NT, 0:NT])
                last.then_inc(s_mtr, 1)

            def tokens(i):
                pe.wait_ge(s_got[i % IN_RING], DMA * (i // IN_RING + 1))
                if i >= 2:
                    pe.wait_ge(s_hr, i - 1)
                transpose_tile(T_PS[i % 2], gathered[i % IN_RING])

            expert = {}

            def load_expert_of(j):
                if j == B:
                    pe.wait_ge(s_eid, 1)
                expert[j] = pe.value_load(expert_of[0:1, j - B:j - B + 1], min_val=0, max_val=EXPERTS - 1)

            def routed_weights(j, row):
                return w_routed[:, bass.ds(expert[j], 1), row, :].rearrange("p e n -> p (e n)")

            def gate_up(j):
                if j < B:
                    pe.wait_ge(s_src[j % 3], DMA * (j // 3 + 1))
                    if j == 0:
                        pe.wait_ge(s_wsh, DMA)
                        pe.wait_ge(s_exp, STEPS * B)
                        pe.wait_ge(s_mx, STEPS * B)
                else:
                    pe.wait_ge(s_hr, j - B + 1)
                    if j == B:
                        pe.wait_ge(s_wrt, EXPERTS * DMA)
                if j >= 2:
                    pe.wait_ge(s_a, j - 1)
                if j < B:
                    for f in range(2 * FF // P):
                        for c in range(CHUNKS):
                            last = nc.tensor.matmul(G_PS[j % 2][:, f * P:(f + 1) * P],
                                                    w_shared[:, c, f * P:(f + 1) * P], h_t[j % 3][:, c, :],
                                                    start=(c == 0), stop=(c == CHUNKS - 1))
                else:
                    for c in range(CHUNKS):
                        last = nc.tensor.matmul(G_PS[j % 2][:], h_t[j % 3][:, c, :], routed_weights(j, c),
                                                start=(c == 0), stop=(c == CHUNKS - 1))
                last.then_inc(s_gu, 1)

            def turn_act(j):
                pe.wait_ge(s_a, j + 1)
                pe.wait_ge(s_at, j - B) if j > B else pe.wait_ge(s_u, 2 * B)
                for f in range(FF // P):
                    last = nc.tensor.transpose(A_PS[:, f * P:(f + 1) * P], act[j % 2][:, f * P:(f + 1) * P], ident[:])
                last.then_inc(s_ta, 1)

            def down(j):
                pe.wait_ge(s_a, j + 1) if j < B else pe.wait_ge(s_at, j - B + 1)
                if j >= 2:
                    if j - 2 < B:
                        pe.wait_ge(s_ysh, j - 1)
                    else:
                        pe.wait_ge(s_yrt, j - 1 - B)
                for f in range(FF // P):
                    w = w_shared[:, CHUNKS + f, :] if j < B else routed_weights(j, CHUNKS + f)
                    last = nc.tensor.matmul(Y_PS[j % 2][:], act_t[j % 2][:, f, :], w,
                                            start=(f == 0), stop=(f == FF // P - 1))
                last.then_inc(s_dn, 1)

            for j in range(JOBS + 1):
                if j in ROUTER_JOBS:
                    turn_tokens(ROUTER_JOBS[j])
                if j == TURN_AT:
                    turn_map()
                if j >= B + 1:
                    turn_act(j - 1)
                if B <= j + 1 < JOBS:
                    tokens(j + 1 - B)
                if j < JOBS:
                    gate_up(j)
                if B <= j + 1 < JOBS:
                    load_expert_of(j + 1)
                if j in ROUTER_JOBS:
                    router_logits(ROUTER_JOBS[j])
                if j == COUNT_AT:
                    count_choices()
                if j >= 1:
                    down(j - 1)


def kernel(**inputs):
    import numpy as np
    from concourse import bacc
    from concourse.bass_utils import run_bass_kernel_spmd

    def attention(name):
        return inputs["L0_xattn_" + name]

    def ffn(name):
        return inputs["L0_ffn_" + name]

    gate = np.concatenate([ffn("sw_gate")[None], ffn("w_gate")])
    up = np.concatenate([ffn("sw_up")[None], ffn("w_up")])
    down = np.concatenate([ffn("sw_down")[None], ffn("w_down")])
    gate_up = np.concatenate([gate, up], axis=2).reshape(EXPERTS + 1, CHUNKS, P, 2 * FF)
    weights = np.concatenate([gate_up, down.reshape(EXPERTS + 1, FF // P, P, L)], axis=1)
    x = inputs["x"]
    arrays = dict(
        x=x, ctx=inputs["ctx_2048"], g_xattn=inputs["g_xattn"].reshape(1, 1), g_ffn=inputs["g_ffn"].reshape(1, 1),
        wq=attention("Wq").T, bq=attention("bq").reshape(P, 1), wk=attention("Wk").T, bk=attention("bk").reshape(P, 1),
        wv=attention("Wv").T, bv=attention("bv").reshape(P, 1), rms=ffn("rms_weight").reshape(1, L),
        router=ffn("router_w"), w=weights.transpose(0, 2, 1, 3))
    arrays = {f"in_{name}": np.ascontiguousarray(value) for name, value in arrays.items()}
    tokens = x.shape[0] * P
    nc = bacc.Bacc("TRN2", target_bir_lowering=False, num_devices=1)
    tensors = [nc.dram_tensor(name, value.shape, mybir.dt.from_np(value.dtype), kind="ExternalInput").ap()
               for name, value in arrays.items()]
    tensors.append(nc.dram_tensor("out", (tokens + P, L), F32, kind="ExternalOutput").ap())
    build(nc, *tensors)
    result = run_bass_kernel_spmd(nc, [arrays], core_ids=[0]).results[0]["out"]
    return result[:tokens].reshape(x.shape)
```

```python
import struct
from contextlib import ExitStack

import concourse.bass as bass
from concourse import mybir

F32 = mybir.dt.float32
BF16 = mybir.dt.bfloat16
ALU = mybir.AluOpType
ACT = mybir.ActivationFunctionType
I32 = mybir.dt.int32
AX_X = mybir.AxisListType.X

P = 128
HEADS = 8
DH = P // HEADS
L = 512
KT = L // P
LN_EPS = 1e-5
RMS_EPS = 1e-6
DMA = 16

HI, MID, LO = range(3)
K_PARTS = (HI, MID, LO, HI, MID, HI)
Q_PARTS = (HI, HI, HI, MID, MID, LO)


def runs(parts):
    out = []
    for at, part in enumerate(parts):
        if out and part == out[-1][1] + out[-1][2]:
            out[-1][2] += 1
        else:
            out.append([at, part, 1])
    return out


READS = len(runs(K_PARTS)) + len(runs(Q_PARTS))
STACK = len(K_PARTS) * DH
SHIFTED = STACK + 2

STEPS = HEADS * KT
PROJECT_AT = {22: (3, 0), 26: (3, 1), 7: (2, 2)}
EVAC_AT = {23: (3, 0), 27: (3, 1), 8: (2, 2)}
HIGH_AT = (25, 29)
MAX_AT = (18, 2)
ROW_AT = (24, 9)
VALUES_LATE = 2
TURN_TOKENS_AT = 10
LOGITS_AT = 14
MOMENTS2_AT = 7
MOMENTS_AT = 23
RECIP_AT = 13
GROUP = 4
EXPERTS = 8
FF = 256
CHUNKS = L // P
IN_RING, OUT_RING = 5, 3
ARENA = 34112
W_ROWS = CHUNKS + FF // P
TWO_ONES = struct.unpack("f", struct.pack("I", 0x3F803F80))[0]
FIRST_BITS = 0x5F3759DF
X_AHEAD = 7


class Arena:

    def __init__(self, tensor, start=0):
        self.tensor, self.at = tensor, start

    def take(self, words, dtype=F32):
        view = self.tensor[:, self.at:self.at + words]
        self.at += words
        return view if dtype == F32 else view.bitcast(dtype)


def build(nc, x_d, ctx_d, g_xattn_d, g_ffn_d, wq_d, bq_d, wk_d, bk_d, wv_d, bv_d, rms_d, router_d, w_d, out_d):
    B = x_d.shape[0]
    T = B * P
    NT = 2 * B + EXPERTS - 1
    es = ExitStack()
    with es:
        def sem(name):
            return es.enter_context(nc.semaphore(name))

        def sb(name, shape, dt=F32):
            return es.enter_context(nc.sbuf_tensor(name, shape, dt))

        def psum(name, shape, dt=F32):
            return es.enter_context(nc.psum_tensor(name, shape, dt))

        def dram(name, shape, dt):
            return nc.dram_tensor(name, shape, dt, kind="Internal").ap()

        xs = sb("xs", [P, B, L])
        arena = sb("arena", [P, ARENA])
        a = Arena(arena)
        q_stack = [a.take(HEADS * L // 2, BF16).rearrange("p (h l) -> p h l", h=HEADS) for _ in range(3)]
        k_stack = [a.take(HEADS * L // 2, BF16).rearrange("p (h l) -> p h l", h=HEADS) for _ in range(3)]
        probs = [a.take(GROUP * L).rearrange("p (j l) -> p j l", j=GROUP) for _ in range(3)]
        v_ones = [a.take(KT * HEADS * 2 * DH).rearrange("p (t h e) -> p t h e", t=KT, h=HEADS) for _ in range(3)]
        ctx_in = [a.take(L) for _ in range(2)]
        xn = [a.take(L) for _ in range(2)]
        proj = [a.take(L) for _ in range(2)]
        rest = a.take(L)
        parts = [[a.take(L // 2, BF16) for _ in range(3)] for _ in range(2)]
        wq, wk, wv = (a.take(P) for _ in range(3))
        attention_end = a.at

        a = Arena(arena)
        w_routed = a.take(EXPERTS * W_ROWS * L).rearrange("p (e r n) -> p e r n", e=EXPERTS, r=W_ROWS)
        hidden = [a.take(FF) for _ in range(2)]
        act_t = [a.take(FF).rearrange("p (c n) -> p c n", c=FF // P) for _ in range(2)]
        h_t = [a.take(L).rearrange("p (c n) -> p c n", c=CHUNKS) for _ in range(3)]
        assert a.at >= attention_end, (a.at, attention_end)
        w_rms = a.take(L)
        act = [w_rms[:, n * FF:(n + 1) * FF] for n in range(2)]

        pv_sb = a.take(2 * L).rearrange("p (g l) -> p g l", g=2)
        pv_num = a.take(L)
        pv_rden = a.take(L)
        den_c = a.take(L * HEADS // P)
        rden_c = a.take(L * HEADS // P)
        tok = a.take(L)
        tok_t = a.take(L).rearrange("p (c n) -> p c n", c=CHUNKS)
        logits = a.take(B * EXPERTS)
        w_shared = a.take(W_ROWS * L).rearrange("p (r n) -> p r n", r=W_ROWS)
        assert a.at <= ARENA, a.at
        gathered = [xs[:, n, :] for n in range(IN_RING)]
        y_sb = [xs[:, IN_RING + n, :] for n in range(OUT_RING)]
        R = B * EXPERTS
        a = Arena(w_routed[:, EXPERTS - 1].rearrange("p r n -> p (r n)"))

        def by_token(v):
            return v.rearrange("p (t e) -> p t e", e=EXPERTS)

        def by_expert(v):
            return v.rearrange("p (e t) -> p e t", e=EXPERTS)

        prob = a.take(R)
        left = a.take(R)
        pick = [a.take(R) for _ in range(2)]
        rank = a.take(R)
        r_tmp = a.take(R)
        place = a.take(R)
        restart = a.take(R)
        le = a.take(NT * EXPERTS)

        bias = sb("bias", [P, 3])
        gates = sb("gates", [P, 2])
        tgates = sb("tgates", [P, 2])
        tg_bv = sb("tg_bv", [P, 1])
        ident = sb("ident", [P, P])
        stats = sb("stats", [P, B, 6])
        mv = sb("mv", [P, B, 2])
        rstd = sb("rstd", [P, B])
        nmr = sb("nmr", [P, B])
        row_max = [sb(f"row_max{i}", [P, HEADS * KT]) for i in range(2)]
        m_rows = [sb(f"m_rows{i}", [GROUP * KT, 2, P], BF16) for i in range(2)]

        mv2 = sb("mv2", [P, B, 2])
        arg = sb("arg", [P, B])
        half_i = sb("half_i", [P, B], I32)
        r2 = sb("r2", [P, B])
        nmr2 = sb("nmr2", [P, B])
        newton = sb("newton", [P, 1])
        w_router = sb("w_router", [P, CHUNKS, EXPERTS])
        before = sb("before", [P, P], BF16)
        ones = sb("ones", [P, P], BF16)
        top = sb("top", [P, 8, B])
        chosen = sb("chosen", [P, R], BF16)
        slots = sb("slots", [P, 2, B], I32)
        meta = sb("meta", [P, 2, B, 2])
        per_e = sb("per_e", [P, 4, EXPERTS])
        per_ei = sb("per_ei", [P, EXPERTS], I32)
        slot_map = sb("slot_map", [NT, P, 2])
        slot_i = sb("slot_i", [P, P], I32)
        ids = sb("ids", [P, NT], I32)
        wts = sb("wts", [P, NT])
        expert_of = sb("expert_of", [P, NT], I32)
        tile_no = sb("tile_no", [P, NT])

        banks = [psum(f"bank{i}", [P, L]) for i in range(8)]
        E_BANKS, M_BANKS = 3, 3
        e_ps = banks[0:E_BANKS]
        m_ps = banks[E_BANKS:E_BANKS + M_BANKS]
        pv_ps, misc_ps = banks[6:8]

        parts_d = [[dram(f"parts_{n}{i}", (HEADS, 3, DH, L), BF16) for i in range(2)] for n in "kq"]
        pv_d = dram("pv_d", (HEADS, 2 * DH, L), F32)
        rden_d = dram("rden_d", (HEADS, L), F32)
        h_d = dram("h_d", (T + P, L), F32)
        ht_d = dram("ht_d", (B, P, L), F32)
        map_d = dram("map_d", (NT * P, 2), F32)

        s_first = sem("s_first")
        s_const = sem("s_const")
        s_setup = sem("s_setup")
        s_ones = sem("s_ones")
        s_x = [sem(f"s_xin{i}") for i in range(4)]
        s_ctx = [sem(f"s_ctx{i}") for i in range(2)]
        s_dve = sem("s_dve")
        s_rstd = sem("s_rstd")
        s_tanh = sem("s_tanh")
        s_gate = sem("s_gate")
        s_pool = sem("s_pool")
        s_xn = sem("s_xn")
        s_proj = sem("s_proj")
        s_evac = sem("s_evac")
        s_hi = sem("s_hi")
        s_part = sem("s_part")
        s_wr = [sem(f"s_wr{i}") for i in range(2)]
        s_rd = [sem(f"s_rd{i}") for i in range(3)]
        s_ms = sem("s_ms")
        s_mx = sem("s_mx")
        s_mt = sem("s_mt")
        s_mr = sem("s_mr")
        s_row = [sem(f"s_row{i}") for i in range(2)]
        s_es = sem("s_es")
        s_exp = sem("s_exp")
        s_pv = sem("s_pv")
        s_u = sem("s_u")
        s_w = sem("s_w")
        s_sc = sem("s_sc")
        s_rc = sem("s_rc")
        s_r = sem("s_r")
        s_fin = sem("s_fin")
        s_x2 = sem("s_x2")
        s_wsh = sem("s_wsh")
        s_wrt = sem("s_wrt")
        s_guess = sem("s_guess")
        s_h = sem("s_h")
        s_hst = sem("s_hst")
        s_wnorm = sem("s_wnorm")
        s_tr = sem("s_tr")
        s_hf = sem("s_hf")
        s_hts = sem("s_hts")
        s_lg = sem("s_lg")
        s_lc = sem("s_lc")
        s_el = sem("s_el")
        s_ex = sem("s_ex")
        s_ch = sem("s_ch")
        s_cnt = sem("s_cnt")
        s_iota = sem("s_iota")
        s_cc = sem("s_cc")
        s_map0 = sem("s_map0")
        s_slot = sem("s_slot")
        s_eid = sem("s_eid")
        s_sc2 = sem("s_sc2")
        s_map = sem("s_map")
        s_mtr = sem("s_mtr")
        s_ids = sem("s_ids")
        s_src = [sem(f"s_src{i}") for i in range(3)]
        s_got = [sem(f"s_got{i}") for i in range(IN_RING)]
        s_hr = sem("s_hr")
        s_gu = sem("s_gu")
        s_si = sem("s_si")
        s_a = sem("s_a")
        s_ta = sem("s_ta")
        s_at = sem("s_at")
        s_dn = sem("s_dn")
        s_ysh = sem("s_ysh")
        s_yrt = sem("s_yrt")
        s_res = [sem(f"s_res{i}") for i in range(2)]
        s_acc = sem("s_acc")

        G_PS = banks[0:2]
        Y_PS = banks[2:4]
        T_PS = banks[4:6]
        A_PS = banks[6]
        R_PS = banks[7]
        JOBS = B + NT
        EXPERT_JOBS = range(5, 5 + 2 * (EXPERTS - 1), 2)
        EXP_AT = 6
        COUNT_AT = 8
        LATE_AT = EXPERT_JOBS.stop
        MAP_AT = B - 4
        TURN_AT = B - 3

        n_const = 4
        TURNS = range(-3, B)
        ROUTER_JOBS = {0: B - 3, 3: B - 2, 5: B - 1}

        def is_b(b):
            return 0 <= b < B

        block = es.enter_context(nc.Block())

        def ones_rows(stack):
            return stack[STACK:SHIFTED, :, :].rearrange("p h l -> p (h l)").bitcast(F32)

        @block.sync
        def _(sp):
            def load(dst, src):
                sp.dma_start(dst, src).then_inc(s_const, DMA)

            def load_x(b):
                if b >= 4:
                    sp.wait_ge(s_rstd, b - 3)
                sp.dma_start(xs[:, b, :], x_d[b]).then_inc(s_x[b % 4], DMA)

            def load_ctx(b):
                if b >= 2:
                    sp.wait_ge(s_proj, 3 * (b - 2) + 3)
                sp.dma_start(ctx_in[b % 2], ctx_d[b]).then_inc(s_ctx[b % 2], DMA)

            def load_first(dst, src):
                sp.dma_start(dst, src).then_inc(s_first, DMA)

            load_ctx(0)
            load_first(wk[:], wk_d)
            for n, v in enumerate((bk_d, bq_d, bv_d)):
                load_first(bias[:, n:n + 1], v)
            load_x(0)
            load(wq[:], wq_d)
            load_ctx(1)
            load(gates[:, 0:1], g_xattn_d.broadcast_to([P, 1]))
            load(gates[:, 1:2], g_ffn_d.broadcast_to([P, 1]))
            load(wv[:], wv_d)
            for b in range(1, X_AHEAD - 3):
                load_x(b)

            def write(b, n, part):
                if b >= 2 and part == HI:
                    sp.wait_ge(s_rd[(b - 2) % 3], READS * DMA * ((b - 2) // 3 + 1))
                if part == HI:
                    sp.wait_ge(s_hi, 2 * b + n + 1)
                else:
                    sp.wait_ge(s_part, 4 * b + 2 * n + part)
                sp.dma_start(parts_d[n][b % 2][:, part, :, :], parts[n][part]).then_inc(s_wr[n], DMA)

            def read(b, n):
                sp.wait_ge(s_wr[n], 3 * DMA * (b + 1))
                if b >= 3 and n == 0:
                    sp.wait_ge(s_es, STEPS * (b - 2))
                src = parts_d[n][b % 2]
                stack = (k_stack, q_stack)[n][b % 3]
                order = (K_PARTS, Q_PARTS)[n]
                for at, part, k in runs(order):
                    sp.dma_start(stack[at * DH:(at + k) * DH, :, :],
                                 src[:, part:part + k].rearrange("h t d l -> (t d) h l")
                                 ).then_inc(s_rd[b % 3], DMA)

            def store_values(b):
                sp.wait_ge(s_u, 2 * b + 2)
                sp.wait_ge(s_fin, 2 * DMA * b)
                sp.dma_start(pv_d.rearrange("(g h) e l -> (h e) g l", g=2), pv_sb).then_inc(s_w, DMA)

            def load_denominators(b):
                sp.wait_ge(s_w, DMA * (b + 1))
                if b:
                    sp.wait_ge(s_rc, b)
                sp.dma_start(den_c, pv_d[:, DH, :].rearrange("h (c w) -> h c w", c=DH)).then_inc(s_sc, DMA)

            def store_reciprocals(b):
                sp.wait_ge(s_rc, b + 1)
                sp.dma_start(rden_d, rden_c).then_inc(s_r, DMA)

            def load_values(b):
                sp.wait_ge(s_r, DMA * (b + 1))
                if b:
                    sp.wait_ge(s_x2, b)
                sp.dma_start(pv_rden, rden_d.unsqueeze(1).broadcast_to([HEADS, DH, L])).then_inc(s_fin, DMA)
                sp.dma_start(pv_num, pv_d[:, 0:DH, :]).then_inc(s_fin, DMA)

            def store_tokens(b):
                sp.wait_ge(s_h, b + 1)
                sp.dma_start(h_d[b * P:(b + 1) * P, :], tok).then_inc(s_hst, DMA)
                if b == 0:
                    sp.dma_start(h_d[T:T + P, :], tok).then_inc(s_hst, DMA)

            def store_turned(b):
                sp.wait_ge(s_hf, b + 1)
                sp.dma_start(ht_d[b], tok_t).then_inc(s_hts, DMA)

            for i in TURNS:
                if is_b(i + 2):
                    read(i + 2, 0)
                if is_b(i - 1):
                    store_values(i - 1)
                if is_b(i + 2):
                    write(i + 2, 1, HI)
                if is_b(i - 1):
                    load_denominators(i - 1)
                if is_b(i + 2):
                    write(i + 2, 1, MID)
                if is_b(i - 1):
                    store_reciprocals(i - 1)
                if is_b(i + 2):
                    write(i + 2, 1, LO)
                if is_b(i + 4) and i + 4 >= 2:
                    load_ctx(i + 4)
                if is_b(i - 3):
                    store_turned(i - 3)
                if is_b(i + 2):
                    read(i + 2, 1)
                if is_b(i - 1):
                    load_values(i - 1)
                if is_b(i - 2):
                    store_tokens(i - 2)
                if is_b(i + 3):
                    for part in (HI, MID, LO):
                        write(i + 3, 0, part)
                if is_b(i + X_AHEAD):
                    load_x(i + X_AHEAD)
                if 2 <= i < 2 + W_ROWS:
                    sp.dma_start(w_shared[:, i - 2, :], w_d[0, :, i - 2, :]).then_inc(s_wsh, DMA)
                if i == 0:
                    sp.dma_start(w_router[:], router_d.rearrange("(c p) e -> p c e", p=P)).then_inc(s_wnorm, DMA)
                    sp.dma_start(w_rms, rms_d.broadcast_to([P, L])).then_inc(s_wnorm, DMA)

            def load_expert(e):
                sp.dma_start(w_routed[:, e], w_d[1 + e]).then_inc(s_wrt, DMA)

            def source(j):
                sp.wait_ge(s_hts, DMA * (j + 1))
                if j >= 3:
                    sp.wait_ge(s_gu, j - 2)
                sp.dma_start(h_t[j % 3], ht_d[j]).then_inc(s_src[j % 3], DMA)

            for j in range(B + 3):
                if j < B:
                    source(j)
                if j == 2:
                    store_values(B - 1)
                    store_turned(B - 3)
                    load_denominators(B - 1)
                if j == 3:
                    store_reciprocals(B - 1)
                if j >= 3:
                    sp.wait_ge(s_ysh, j - 2)
                    sp.dma_start(out_d[(j - 3) * P:(j - 2) * P, :], xs[:, j - 3, :]
                                 ).then_inc(s_res[j - 3 >= IN_RING + OUT_RING], DMA)
                if j == 3:
                    sp.dma_start(out_d[T:T + P, :], xs[:, 0, :]).then_inc(s_res[0], DMA)
                    store_tokens(B - 2)
                    load_values(B - 1)
                if j == 6:
                    store_turned(B - 2)
                    sp.wait_ge(s_cc, 1)
                    sp.dma_start(map_d.rearrange("(n s) k -> n s k", s=P), slot_map[:]).then_inc(s_map0, DMA)
                if j == 7:
                    store_tokens(B - 1)
                if j == 8:
                    store_turned(B - 1)
                if j in EXPERT_JOBS:
                    load_expert(EXPERT_JOBS.index(j))
                if j == LATE_AT:
                    sp.wait_ge(s_eid, 1)
                    load_expert(EXPERTS - 1)
                if j == MAP_AT:
                    sp.wait_ge(s_sc2, 2 * B * DMA)
                    sp.dma_start(slot_map[:], map_d.rearrange("(n s) k -> n s k", s=P)).then_inc(s_map, DMA)
            sp.wait_ge(s_acc, NT * DMA)

        @block.gpsimd
        def _(pool):
            links = [0]

            def link(ins):
                links[0] += 1
                ins.then_inc(s_pool, 1)
                pool.wait_ge(s_pool, links[0])

            link(nc.gpsimd.memset(ident[:], 0.0))
            nc.gpsimd.affine_select(out=ident[:], in_=ident[:], compare_op=ALU.not_equal, fill=1.0, base=0,
                                    pattern=[[-1, P]], channel_multiplier=1).then_inc(s_setup, 1)

            def refine(r, b):
                for _ in range(3):
                    link(nc.gpsimd.tensor_scalar(newton[:], r, r, arg[:, b:b + 1], ALU.mult, ALU.mult))
                    link(nc.gpsimd.tensor_scalar(newton[:], newton[:], -0.5, 1.5, ALU.mult, ALU.add))
                    link(nc.gpsimd.tensor_tensor(r, r, newton[:], ALU.mult))

            def normalise(b):
                pool.wait_ge(s_rstd, b + 1)
                refine(rstd[:, b:b + 1], b)
                link(nc.gpsimd.tensor_scalar(nmr[:, b:b + 1], mv[:, b, 0:1], rstd[:, b:b + 1], -1.0,
                                             ALU.mult, ALU.mult))
                if b >= 2:
                    pool.wait_ge(s_proj, 3 * (b - 2) + 2)
                nc.gpsimd.tensor_scalar(xn[b % 2], xs[:, b, :], rstd[:, b:b + 1], nmr[:, b:b + 1],
                                        ALU.mult, ALU.add).then_inc(s_xn, 1)

            def split(b, n):
                pool.wait_ge(s_hi, 2 * b + n + 1)
                pool.wait_ge(s_part, 4 * b + 2 * n)
                pool.wait_ge(s_wr[n], 3 * DMA * b)
                hi, mid, lo = parts[n]
                nc.gpsimd.tensor_tensor(mid, proj[n], hi, ALU.subtract).then_inc(s_part, 1)
                link(nc.gpsimd.tensor_tensor(rest, proj[n], hi, ALU.subtract))
                pool.wait_ge(s_part, 4 * b + 2 * n + 1)
                nc.gpsimd.tensor_tensor(lo, rest, mid, ALU.subtract).then_inc(s_part, 1)
                pool.wait_ge(s_part, 4 * b + 2 * n + 2)

            def add_attention(b):
                pool.wait_ge(s_fin, 2 * DMA * (b + 1))
                if b == 0:
                    pool.wait_ge(s_gate, 1)
                link(nc.gpsimd.tensor_tensor(pv_num, pv_num, pv_rden, ALU.mult))
                link(nc.gpsimd.tensor_scalar(pv_num, pv_num, tgates[:, 0:1], tg_bv[:], ALU.mult, ALU.add))
                nc.gpsimd.tensor_tensor(xs[:, b, :], xs[:, b, :], pv_num, ALU.add).then_inc(s_x2, 1)
                pool.wait_ge(s_x2, b + 1)

            link(nc.gpsimd.memset(before[:], 1.0))
            nc.gpsimd.affine_select(out=before[:], in_=before[:], compare_op=ALU.is_gt, fill=0.0, base=0,
                                    pattern=[[1, P]], channel_multiplier=-1).then_inc(s_setup, 1)
            nc.gpsimd.memset(ones[:], 1.0).then_inc(s_setup, 1)
            nc.gpsimd.iota(slot_i[:], pattern=[[1, P]], base=T, channel_multiplier=0).then_inc(s_setup, 1)

            def tokens(b):
                pool.wait_ge(s_guess, b + 1)
                r = r2[:, b:b + 1]
                refine(r, b)
                link(nc.gpsimd.tensor_scalar(nmr2[:, b:b + 1], mv2[:, b, 0:1], r, -1.0, ALU.mult, ALU.mult))
                if b:
                    pool.wait_ge(s_tr, b)
                    pool.wait_ge(s_hst, DMA * (b + 1))
                else:
                    pool.wait_ge(s_wnorm, 2 * DMA)
                link(nc.gpsimd.tensor_scalar(tok, xs[:, b, :], r, nmr2[:, b:b + 1], ALU.mult, ALU.add))
                nc.gpsimd.tensor_tensor(tok, tok, w_rms, ALU.mult).then_inc(s_h, 1)
                pool.wait_ge(s_h, b + 1)

            normalise(0)
            for v, k in zip(v_ones[1:], k_stack[1:]):
                link(nc.gpsimd.memset(v[:, :, :, DH:], 1.0))
                link(nc.gpsimd.memset(ones_rows(k), TWO_ONES))
            for i in TURNS:
                if is_b(i + 2) and i + 2 > 0:
                    split(i + 2, 1)
                if is_b(i + 4):
                    normalise(i + 4)
                if is_b(i - 2):
                    tokens(i - 2)
                if is_b(i + 3) and i + 3 > 0:
                    split(i + 3, 0)
                if is_b(i - 1):
                    add_attention(i - 1)
            tokens(B - 2)
            add_attention(B - 1)
            tokens(B - 1)

            for out, pattern, base, cm in (
                    (by_token(rank), [[0, B], [-1, EXPERTS]], EXPERTS, 0),
                    (tile_no[:], [[1, NT]], 0, 0),
                    (top[:, 7, :], [[P, B]], 0, 1)):
                nc.gpsimd.iota(out.bitcast(I32), pattern=pattern, base=base, channel_multiplier=cm).then_inc(s_iota, 1)

            pool.wait_ge(s_map0, DMA)
            for k in range(2):
                pool.wait_ge(s_slot, k + 1)
                for t in range(B):
                    nc.gpsimd.indirect_dma_start(
                        map_d, bass.IndirectOffsetOnAxis(ap=slots[:, k, t:t + 1], axis=0),
                        meta[:, k, t, :], None).then_inc(s_sc2, DMA)
            def gather(i):
                if i >= IN_RING:
                    pool.wait_ge(s_tr, B + i - IN_RING + 1)
                nc.gpsimd.indirect_dma_start(gathered[i % IN_RING], None, h_d,
                                             bass.IndirectOffsetOnAxis(ap=ids[:, i:i + 1], axis=0)
                                             ).then_inc(s_got[i % IN_RING], DMA)

            def add_to_output(i):
                pool.wait_ge(s_yrt, i + 1)
                pool.wait_ge(s_acc, DMA * i)
                nc.gpsimd.indirect_dma_start(out_d, bass.IndirectOffsetOnAxis(ap=ids[:, i:i + 1], axis=0),
                                             y_sb[i % OUT_RING], None, compute_op=ALU.add).then_inc(s_acc, DMA)

            pool.wait_ge(s_ids, 1)
            pool.wait_ge(s_hst, DMA * (B + 1))
            first = min(B, IN_RING + OUT_RING)
            pool.wait_ge(s_res[0], (first + 1) * DMA)
            for i in range(IN_RING):
                gather(i)
            pool.wait_ge(s_res[1], (B - first) * DMA)
            for i in range(NT):
                if i and i - 1 + IN_RING < NT:
                    gather(i - 1 + IN_RING)
                add_to_output(i)

        @block.vector
        def _(dve):
            links = [0]

            def link(ins):
                links[0] += 1
                ins.then_inc(s_dve, 1)
                dve.wait_ge(s_dve, links[0])

            def chain(*ops):
                for n, op in enumerate(ops):
                    if n:
                        dve.wait_ge(s_dve, done)
                        yield
                    ins = op()
                    if n < len(ops) - 1:
                        links[0] += 1
                        done = links[0]
                        ins.then_inc(s_dve, 1)

            def run(steps):
                for _ in steps:
                    pass

            def first_value(r, b):
                half = half_i[:, b:b + 1]
                return (lambda: nc.vector.tensor_single_scalar(half, arg[:, b:b + 1].bitcast(I32), 1,
                                                               ALU.arith_shift_right),
                        lambda: nc.vector.tensor_scalar(r.bitcast(I32), half, -1.0, float(FIRST_BITS),
                                                        ALU.mult, ALU.add))

            def moments(b):
                dve.wait_ge(s_x[b % 4], DMA * (b // 4 + 1))
                shift, first = first_value(rstd[:, b:b + 1], b)
                return chain(lambda: nc.vector.bn_stats(stats[:, b, :], xs[:, b, :]),
                             lambda: nc.vector.bn_aggr(mv[:, b, :], stats[:, b, :]),
                             lambda: nc.vector.tensor_scalar_add(arg[:, b:b + 1], mv[:, b, 1:2], LN_EPS),
                             shift, lambda: first().then_inc(s_rstd, 1))

            def moments2(b):
                dve.wait_ge(s_x2, b + 1)
                shift, first = first_value(r2[:, b:b + 1], b)
                return chain(lambda: nc.vector.bn_stats(stats[:, b, :], xs[:, b, :]),
                             lambda: nc.vector.bn_aggr(mv2[:, b, :], stats[:, b, :]),
                             lambda: nc.vector.tensor_scalar(arg[:, b:b + 1], mv2[:, b, 1:2], 1.0 + RMS_EPS,
                                                             LN_EPS * RMS_EPS, ALU.mult, ALU.add),
                             shift, lambda: first().then_inc(s_guess, 1))

            def split_first(n):
                dve.wait_ge(s_hi, n + 1)
                if n:
                    dve.wait_ge(s_part, 2)
                hi, mid, lo = parts[n]
                nc.vector.tensor_tensor(mid, proj[n], hi, ALU.subtract).then_inc(s_part, 1)
                link(nc.vector.tensor_tensor(rest, proj[n], hi, ALU.subtract))
                dve.wait_ge(s_part, 2 * n + 1)
                nc.vector.tensor_tensor(lo, rest, mid, ALU.subtract).then_inc(s_part, 1)

            def take_logits(b):
                dve.wait_ge(s_lg, b + 1)
                nc.vector.tensor_copy(logits[:, b * EXPERTS:(b + 1) * EXPERTS], misc_ps[:, 0:EXPERTS]
                                      ).then_inc(s_lc, 1)

            def invert(b):
                dve.wait_ge(s_sc, DMA * (b + 1))
                if b:
                    dve.wait_ge(s_r, DMA * b)
                nc.vector.reciprocal(rden_c, den_c).then_inc(s_rc, 1)

            def maximum(b, u):
                dve.wait_ge(s_ms, STEPS * b + u + 1)
                if u == 0 and b >= 2:
                    dve.wait_ge(s_mt, 2 * (b - 2) + 2)
                nc.vector.reduce_max(row_max[b % 2][:, u:u + 1], m_ps[(STEPS * b + u) % M_BANKS][:], AX_X).then_inc(s_mx, 1)

            def maxima_rows(b, half):
                n = GROUP * KT
                dve.wait_ge(s_mt, 2 * b + half + 1)
                if b:
                    dve.wait_ge(s_row[half], 2 * DMA * b)
                return chain(
                    lambda: nc.vector.tensor_scalar(m_rows[half][:, 0, :], misc_ps[0:n, 0:P], -1.0, None, ALU.mult),
                    lambda: nc.vector.scalar_tensor_tensor(m_rows[half][:, 1, :], misc_ps[0:n, 0:P], -1.0,
                                                           m_rows[half][:, 0, :], ALU.mult, ALU.subtract
                                                           ).then_inc(s_mr, 1))

            run(moments(0))
            split_first(0)
            nc.vector.memset(v_ones[0][:, :, :, DH:], 1.0).then_inc(s_ones, 1)
            split_first(1)
            run(moments(1))
            nc.vector.memset(ones_rows(k_stack[0]), TWO_ONES).then_inc(s_ones, 1)
            dve.wait_ge(s_tanh, 1)
            dve.wait_ge(s_first, 4 * DMA)
            nc.vector.tensor_tensor(tg_bv[:], tgates[:, 0:1], bias[:, 2:3], ALU.mult).then_inc(s_gate, 1)
            begun = []
            for i in TURNS:
                for s in range(STEPS):
                    if is_b(i + 1):
                        maximum(i + 1, s)
                    if s == MAX_AT[1] + 1 and is_b(i):
                        begun.append(maxima_rows(i, 1))
                    if s == RECIP_AT and is_b(i - 1):
                        invert(i - 1)
                    if s == MAX_AT[0] + 1 and is_b(i + 1):
                        begun.append(maxima_rows(i + 1, 0))
                    if s == MOMENTS_AT and is_b(i + 5):
                        begun.append(moments(i + 5))
                    if s == MOMENTS2_AT and is_b(i - 2):
                        begun.append(moments2(i - 2))
                    if s == LOGITS_AT + 1 and is_b(i - 3):
                        take_logits(i - 3)
                    begun = [steps for steps in begun if next(steps, steps) is not steps]

            TT = nc.vector.tensor_tensor

            def each(v):
                return v.unsqueeze(2).broadcast_to([P, B, EXPERTS])

            def routing():
                dve.wait_ge(s_iota, 3)
                for v in (rank, tile_no[:]):
                    link(nc.vector.tensor_copy(v, v.bitcast(I32)))
                for k in range(2):
                    link(nc.vector.tensor_copy(meta[:, k, :, 0], top[:, 7, :].bitcast(I32)))
                dve.wait_ge(s_setup, 4)
                link(nc.vector.tensor_copy(slot_map[:, :, 0], slot_i[0:NT, :]))
                nc.vector.memset(slot_map[:, :, 1], 0.0).then_inc(s_cc, 1)
                link(nc.vector.memset(restart, 1.0))
                link(nc.vector.memset(by_expert(restart)[:, :, 0:1], 0.0))

                yield
                logits_t = by_token(logits)
                dve.wait_ge(s_lc, B)
                link(nc.vector.reduce_max(top[:, 0, :], logits_t, AX_X))
                TT(by_token(left), logits_t, each(top[:, 0, :]), ALU.subtract).then_inc(s_el, 1)
                yield
                dve.wait_ge(s_ex, 1)
                link(nc.vector.reduce_sum(top[:, 1, :], by_token(prob), AX_X))
                link(nc.vector.reciprocal(top[:, 1, :], top[:, 1, :]))
                link(TT(by_token(prob), by_token(prob), each(top[:, 1, :]), ALU.mult))

                def choose(k, p):
                    link(nc.vector.reduce_max(top[:, 2 + k, :], by_token(p), AX_X))
                    link(TT(by_token(r_tmp), by_token(p), each(top[:, 2 + k, :]), ALU.is_equal))
                    link(TT(r_tmp, r_tmp, rank, ALU.mult))
                    link(nc.vector.reduce_max(top[:, 4, :], by_token(r_tmp), AX_X))
                    link(TT(by_token(pick[k]), by_token(rank), each(top[:, 4, :]), ALU.is_equal))

                choose(0, prob)
                link(nc.vector.scalar_tensor_tensor(left, pick[0], -2.0, prob, ALU.mult, ALU.add))
                yield
                choose(1, left)
                link(TT(by_expert(chosen[:]).rearrange("p e t -> p t e"), by_token(pick[0]), by_token(pick[1]), ALU.add))
                TT(top[:, 5, :], top[:, 2, :], top[:, 3, :], ALU.add).then_inc(s_ch, 1)
                yield
                dve.wait_ge(s_ch, 1)
                link(nc.vector.reciprocal(top[:, 5, :], top[:, 5, :]))
                for k in range(2):
                    link(TT(meta[:, k, :, 1], top[:, 2 + k, :], top[:, 5, :], ALU.mult))
                dve.wait_ge(s_cnt, 1)
                in_tile, totals = R_PS[:, 0:R], R_PS[:, R:2 * R]
                link(nc.vector.tensor_tensor_scan(place, restart, totals, 0.0, ALU.mult, ALU.add))
                link(nc.vector.tensor_scalar_add(per_ei[:], by_expert(place)[:, :, B - 1], float(P - 1)))
                shift = P.bit_length() - 1
                link(nc.vector.tensor_single_scalar(per_ei[:], per_ei[:], shift, ALU.arith_shift_right))
                link(nc.vector.tensor_copy(per_e[:, 0, :], per_ei[:]))
                link(nc.vector.memset(per_e[:, 3, :], 1.0))
                link(nc.vector.tensor_tensor_scan(per_e[:, 1, :], per_e[:, 3, :], per_e[:, 0, :], 0.0, ALU.mult, ALU.add))
                link(TT(per_e[:, 2, :], per_e[:, 1, :], per_e[:, 0, :], ALU.subtract))
                link(nc.vector.tensor_scalar(per_e[:, 2, :], per_e[:, 2, :], float(P), None, ALU.mult))
                link(TT(place, place, totals, ALU.subtract))
                link(TT(place, place, in_tile, ALU.add))
                link(TT(by_expert(place), by_expert(place), per_e[:, 2, :].unsqueeze(2).broadcast_to([P, EXPERTS, B]),
                        ALU.add))
                for k in range(2):
                    link(TT(by_token(r_tmp), by_token(pick[k]), by_expert(place).rearrange("p e t -> p t e"), ALU.mult))
                    link(nc.vector.reduce_sum(top[:, 6, :], by_token(r_tmp), AX_X))
                    nc.vector.tensor_copy(slots[:, k, :], top[:, 6, :]).then_inc(s_slot, 1)
                    dve.wait_ge(s_slot, k + 1)
                    if k == 0:
                        yield
                yield
                le_v = le.rearrange("p (n e) -> p n e", e=EXPERTS)
                link(TT(le_v, per_e[:, 1, :].unsqueeze(1).broadcast_to([P, NT, EXPERTS]),
                        tile_no[:].unsqueeze(2).broadcast_to([P, NT, EXPERTS]), ALU.is_le))
                link(nc.vector.reduce_sum(tile_no[:], le_v, AX_X))
                nc.vector.tensor_scalar(expert_of[:], tile_no[:], float(EXPERTS - 1), None, ALU.min
                                        ).then_inc(s_eid, 1)

            def take_tokens(i):
                dve.wait_ge(s_tr, B + i + 1)
                dve.wait_ge(s_gu, B + i - 2)
                nc.vector.tensor_copy(h_t[(B + i) % 3].rearrange("p c n -> p (c n)"), T_PS[i % 2][:]).then_inc(s_hr, 1)

            def times_up(j):
                dve.wait_ge(s_si, j + 1)
                if j < B:
                    out = act_t[j % 2].rearrange("p c n -> p (c n)")
                    if j >= 2:
                        dve.wait_ge(s_dn, j - 1)
                else:
                    out = act[j % 2]
                    if j >= B + 2:
                        dve.wait_ge(s_ta, j - B - 1)
                nc.vector.tensor_tensor(out, hidden[j % 2], G_PS[j % 2][:, FF:2 * FF], ALU.mult).then_inc(s_a, 1)

            def add_shared(j):
                dve.wait_ge(s_dn, j + 1)
                nc.vector.scalar_tensor_tensor(xs[:, j, :], Y_PS[j % 2][:], tgates[:, 1:2], xs[:, j, :],
                                               ALU.mult, ALU.add).then_inc(s_ysh, 1)

            pieces = routing()
            for j in range(JOBS + 1):
                if j == 1:
                    invert(B - 1)
                if j == 3:
                    run(moments2(B - 1))
                if B <= j + 1 < JOBS:
                    take_tokens(j + 1 - B)
                if j < JOBS:
                    times_up(j)
                if j == 0:
                    run(moments2(B - 2))
                if j in ROUTER_JOBS:
                    take_logits(ROUTER_JOBS[j])
                if 1 <= j <= B:
                    add_shared(j - 1)
                if j >= 4:
                    next(pieces, None)
                if j == TURN_AT:
                    dve.wait_ge(s_mtr, 1)
                    link(nc.vector.tensor_copy(ids[:], R_PS[:, 0:NT]))
                    nc.vector.tensor_scalar(wts[:], R_PS[:, P:P + NT], tgates[:, 1:2], None,
                                            ALU.mult).then_inc(s_ids, 1)

        @block.scalar
        def _(act_e):
            def evacuate(b, n):
                act_e.wait_ge(s_proj, 3 * b + n + 1)
                if b == 0 and n == 0:
                    act_e.wait_ge(s_first, 4 * DMA)
                if n < 2:
                    if b:
                        act_e.wait_ge(s_part, 4 * (b - 1) + 2 * n + 2)
                        act_e.wait_ge(s_wr[n], 3 * DMA * b)
                    nc.scalar.activation(proj[n], misc_ps[:], ACT.Identity, bias=bias[:, n:n + 1]).then_inc(s_evac, 1)
                    return
                if b >= 3:
                    act_e.wait_ge(s_pv, 8 * (b - 2))
                nc.scalar.copy(v_ones[b % 3][:, :, :, 0:DH],
                               misc_ps[:].rearrange("p (t h d) -> p t h d", t=KT, h=HEADS)).then_inc(s_evac, 1)

            def high_part(b, n):
                act_e.wait_ge(s_evac, 3 * b + n + 1)
                nc.scalar.copy(parts[n][HI], proj[n]).then_inc(s_hi, 1)

            def exponential(b, s):
                n = STEPS * b + s
                act_e.wait_ge(s_es, n + 1)
                group, j = divmod(n, GROUP)
                if j == 0 and group >= 3:
                    act_e.wait_ge(s_pv, group - 2)
                nc.scalar.activation(probs[group % 3][:, j, :], e_ps[n % E_BANKS][:], ACT.Exp,
                                     scale=float(DH) ** -0.5).then_inc(s_exp, 1)

            def take_values(b, g):
                act_e.wait_ge(s_pv, 8 * b + 4 * g + 4)
                if b:
                    act_e.wait_ge(s_w, DMA * b)
                nc.scalar.copy(pv_sb[:, g, :], pv_ps[:]).then_inc(s_u, 1)

            def take_turned(b):
                act_e.wait_ge(s_tr, b + 1)
                if b:
                    act_e.wait_ge(s_lg, b)
                    act_e.wait_ge(s_hts, DMA * b)
                nc.scalar.copy(tok_t.rearrange("p c n -> p (c n)"), misc_ps[:]).then_inc(s_hf, 1)

            def row(b, half):
                act_e.wait_ge(s_mr, 2 * b + half + 1)
                for n in range(2):
                    act_e.dma_start(q_stack[b % 3][STACK + n:STACK + n + 1, half * GROUP:(half + 1) * GROUP, :],
                                    m_rows[half][:, n, :]).then_inc(s_row[half], DMA)

            for i in TURNS:
                if i == -2:
                    act_e.wait_ge(s_const, n_const * DMA)
                    nc.scalar.activation(tgates[:], gates[:], ACT.Tanh).then_inc(s_tanh, 1)
                for s in range(STEPS):
                    if is_b(i):
                        exponential(i, s)
                    if s == ROW_AT[1] and is_b(i):
                        row(i, 1)
                    if s == ROW_AT[0] and is_b(i + 1):
                        row(i + 1, 0)
                    if s in HIGH_AT and is_b(i + 3):
                        high_part(i + 3, HIGH_AT.index(s))
                    if s == TURN_TOKENS_AT + 1 and is_b(i - 3):
                        take_turned(i - 3)
                    if s == VALUES_LATE + 1 and is_b(i - 1):
                        take_values(i - 1, 1)
                    if s == STEPS // 2 + VALUES_LATE + 1 and is_b(i):
                        take_values(i, 0)
                    if s in EVAC_AT and is_b(i + EVAC_AT[s][0]):
                        evacuate(i + EVAC_AT[s][0], EVAC_AT[s][1])

            take_values(B - 1, 1)

            def silu(j):
                act_e.wait_ge(s_gu, j + 1)
                if j >= 2:
                    act_e.wait_ge(s_a, j - 1)
                nc.scalar.activation(hidden[j % 2], G_PS[j % 2][:, 0:FF], ACT.Silu).then_inc(s_si, 1)

            def weigh(i):
                j = B + i
                act_e.wait_ge(s_dn, j + 1)
                if i == 0:
                    act_e.wait_ge(s_ids, 1)
                if i == 0:
                    act_e.wait_ge(s_res[0], (min(B, IN_RING + OUT_RING) + 1) * DMA)
                if i >= OUT_RING:
                    act_e.wait_ge(s_acc, DMA * (i - OUT_RING + 1))
                nc.scalar.activation(y_sb[i % OUT_RING], Y_PS[j % 2][:], ACT.Copy, scale=wts[:, i:i + 1]).then_inc(s_yrt, 1)

            def take_act(j):
                act_e.wait_ge(s_ta, j - B + 1)
                act_e.wait_ge(s_dn, j - 1)
                nc.scalar.copy(act_t[j % 2].rearrange("p c n -> p (c n)"), A_PS[:, 0:FF]).then_inc(s_at, 1)

            for j in range(JOBS + 1):
                if j in ROUTER_JOBS:
                    take_turned(ROUTER_JOBS[j])
                if j == EXP_AT:
                    act_e.wait_ge(s_el, 1)
                    nc.scalar.activation(prob, left, ACT.Exp).then_inc(s_ex, 1)
                if j >= B + 1:
                    take_act(j - 1)
                if j < JOBS:
                    silu(j)
                if j >= B + 1:
                    weigh(j - B - 1)

        @block.tensor
        def _(pe):
            misc_reader = [None]

            def take_misc(reader, count):
                if misc_reader[0]:
                    pe.wait_ge(*misc_reader[0])
                misc_reader[0] = (reader, count)

            def project(b, n):
                take_misc(s_evac, 3 * b + n + 1)
                if n == 0:
                    pe.wait_ge(s_ctx[b % 2], DMA * (b // 2 + 1))
                    if b == 0:
                        pe.wait_ge(s_first, 4 * DMA)
                if n == 1:
                    pe.wait_ge(s_xn, b + 1)
                    if b == 0:
                        pe.wait_ge(s_const, n_const * DMA)
                if n < 2:
                    nc.tensor.matmul(misc_ps[:], (wk, wq)[n][:], ctx_in[b % 2] if n == 0 else xn[b % 2],
                                     start=True, stop=True).then_inc(s_proj, 1)
                    return
                for t in range(KT):
                    last = nc.tensor.matmul(misc_ps[:, t * P:(t + 1) * P], ctx_in[b % 2][:, t * P:(t + 1) * P], wv[:],
                                            start=True, stop=True)
                last.then_inc(s_proj, 1)

            def max_scores(b, u):
                h, qt = divmod(u, KT)
                n = STEPS * b + u
                if u == 0:
                    pe.wait_ge(s_rd[b % 3], READS * DMA * (b // 3 + 1))
                if n >= M_BANKS:
                    pe.wait_ge(s_mx, n - M_BANKS + 1)
                nc.tensor.matmul(m_ps[n % M_BANKS][:], q_stack[b % 3][0:STACK, h, qt * P:(qt + 1) * P],
                                 k_stack[b % 3][0:STACK, h, :], start=True, stop=True).then_inc(s_ms, 1)

            def turn_maxima(b, half):
                n = GROUP * KT
                if b == 0 and half == 0:
                    pe.wait_ge(s_setup, 1)
                pe.wait_ge(s_mx, STEPS * b + n * (half + 1))
                take_misc(s_mr, 2 * b + half + 1)
                nc.tensor.transpose(misc_ps[0:n, 0:P], row_max[b % 2][:, n * half:n * (half + 1)],
                                    ident[:]).then_inc(s_mt, 1)

            def exp_scores(b, s):
                g, kt, j = s // (GROUP * KT), s // GROUP % KT, s % GROUP
                h = GROUP * g + j
                n = STEPS * b + s
                if kt == 0 and j == 0:
                    pe.wait_ge(s_row[g], 2 * DMA * (b + 1))
                if n == 0:
                    pe.wait_ge(s_ones, 2)
                if n >= E_BANKS:
                    pe.wait_ge(s_exp, n - E_BANKS + 1)
                nc.tensor.matmul(e_ps[n % E_BANKS][:], k_stack[b % 3][0:SHIFTED, h, kt * P:(kt + 1) * P],
                                 q_stack[b % 3][0:SHIFTED, h, :], start=True, stop=True).then_inc(s_es, 1)

            def transpose_tile(out, src):
                for c in range(CHUNKS):
                    last = nc.tensor.transpose(out[:, c * P:(c + 1) * P], src[:, c * P:(c + 1) * P], ident[:])
                last.then_inc(s_tr, 1)

            def turn_tokens(b):
                take_misc(s_hf, b + 1)
                pe.wait_ge(s_h, b + 1)
                transpose_tile(misc_ps, tok)

            def router_logits(b):
                take_misc(s_lc, b + 1)
                for c in range(CHUNKS):
                    last = nc.tensor.matmul(misc_ps[:, 0:EXPERTS], tok_t[:, c, :], w_router[:, c, :],
                                            start=(c == 0), stop=(c == CHUNKS - 1))
                last.then_inc(s_lg, 1)

            def values(b, r):
                g, kt = divmod(r, KT)
                pair = 8 * b + r
                pe.wait_ge(s_exp, STEPS * b + GROUP * (r + 1))
                if r == 0:
                    pe.wait_ge(s_evac, 3 * b + 3)
                if kt == 0 and pair:
                    pe.wait_ge(s_u, pair // KT)
                for j in range(GROUP):
                    last = nc.tensor.matmul(pv_ps[2 * DH * j:2 * DH * (j + 1), :], v_ones[b % 3][:, kt, GROUP * g + j, :],
                                            probs[pair % 3][:, j, :], start=(kt == 0), stop=(kt == KT - 1))
                last.then_inc(s_pv, 1)

            for i in TURNS:
                for s in range(STEPS):
                    if is_b(i):
                        exp_scores(i, s)
                    if is_b(i + 1):
                        max_scores(i + 1, s)
                    if s % GROUP == VALUES_LATE:
                        if s < GROUP and is_b(i - 1):
                            values(i - 1, STEPS // GROUP - 1)
                        if s >= GROUP and is_b(i):
                            values(i, s // GROUP - 1)
                    if s == MAX_AT[1] and is_b(i):
                        turn_maxima(i, 1)
                    if s == MAX_AT[0] and is_b(i + 1):
                        turn_maxima(i + 1, 0)
                    if s == TURN_TOKENS_AT and is_b(i - 3):
                        turn_tokens(i - 3)
                    if s == LOGITS_AT and is_b(i - 3):
                        router_logits(i - 3)
                    if s in PROJECT_AT and is_b(i + PROJECT_AT[s][0]):
                        project(i + PROJECT_AT[s][0], PROJECT_AT[s][1])

            values(B - 1, STEPS // GROUP - 1)

            def count_choices():
                pe.wait_ge(s_ch, 1)
                pe.wait_ge(s_setup, 4)
                nc.tensor.matmul(R_PS[:, 0:R], before[:], chosen[:], start=True, stop=True)
                nc.tensor.matmul(R_PS[:, R:2 * R], ones[:], chosen[:], start=True, stop=True).then_inc(s_cnt, 1)

            def turn_map():
                pe.wait_ge(s_map, DMA)
                for n in range(2):
                    last = nc.tensor.transpose(R_PS[:, n * P:n * P + NT], slot_map[:, :, n], ident[0:NT, 0:NT])
                last.then_inc(s_mtr, 1)

            def tokens(i):
                pe.wait_ge(s_got[i % IN_RING], DMA * (i // IN_RING + 1))
                if i >= 2:
                    pe.wait_ge(s_hr, i - 1)
                transpose_tile(T_PS[i % 2], gathered[i % IN_RING])

            expert = {}

            def load_expert_of(j):
                if j == B:
                    pe.wait_ge(s_eid, 1)
                expert[j] = pe.value_load(expert_of[0:1, j - B:j - B + 1], min_val=0, max_val=EXPERTS - 1)

            def routed_weights(j, row):
                return w_routed[:, bass.ds(expert[j], 1), row, :].rearrange("p e n -> p (e n)")

            def gate_up(j):
                if j < B:
                    pe.wait_ge(s_src[j % 3], DMA * (j // 3 + 1))
                    if j == 0:
                        pe.wait_ge(s_wsh, W_ROWS * DMA)
                        pe.wait_ge(s_exp, STEPS * B)
                        pe.wait_ge(s_mx, STEPS * B)
                else:
                    pe.wait_ge(s_hr, j - B + 1)
                    if j == B:
                        pe.wait_ge(s_wrt, EXPERTS * DMA)
                if j >= 2:
                    pe.wait_ge(s_a, j - 1)
                if j < B:
                    for f in range(2 * FF // P):
                        for c in range(CHUNKS):
                            last = nc.tensor.matmul(G_PS[j % 2][:, f * P:(f + 1) * P],
                                                    w_shared[:, c, f * P:(f + 1) * P], h_t[j % 3][:, c, :],
                                                    start=(c == 0), stop=(c == CHUNKS - 1))
                else:
                    for c in range(CHUNKS):
                        last = nc.tensor.matmul(G_PS[j % 2][:], h_t[j % 3][:, c, :], routed_weights(j, c),
                                                start=(c == 0), stop=(c == CHUNKS - 1))
                last.then_inc(s_gu, 1)

            def turn_act(j):
                pe.wait_ge(s_a, j + 1)
                pe.wait_ge(s_at, j - B) if j > B else pe.wait_ge(s_u, 2 * B)
                for f in range(FF // P):
                    last = nc.tensor.transpose(A_PS[:, f * P:(f + 1) * P], act[j % 2][:, f * P:(f + 1) * P], ident[:])
                last.then_inc(s_ta, 1)

            def down(j):
                pe.wait_ge(s_a, j + 1) if j < B else pe.wait_ge(s_at, j - B + 1)
                if j >= 2:
                    if j - 2 < B:
                        pe.wait_ge(s_ysh, j - 1)
                    else:
                        pe.wait_ge(s_yrt, j - 1 - B)
                for f in range(FF // P):
                    w = w_shared[:, CHUNKS + f, :] if j < B else routed_weights(j, CHUNKS + f)
                    last = nc.tensor.matmul(Y_PS[j % 2][:], act_t[j % 2][:, f, :], w,
                                            start=(f == 0), stop=(f == FF // P - 1))
                last.then_inc(s_dn, 1)

            for j in range(JOBS + 1):
                if j in ROUTER_JOBS:
                    turn_tokens(ROUTER_JOBS[j])
                if j == TURN_AT:
                    turn_map()
                if j >= B + 1:
                    turn_act(j - 1)
                if B <= j + 1 < JOBS:
                    tokens(j + 1 - B)
                if j < JOBS:
                    gate_up(j)
                if B <= j + 1 < JOBS:
                    load_expert_of(j + 1)
                if j >= 1:
                    down(j - 1)
                if j in ROUTER_JOBS:
                    router_logits(ROUTER_JOBS[j])
                if j == COUNT_AT:
                    count_choices()


def kernel(**inputs):
    import numpy as np
    from concourse import bacc
    from concourse.bass_utils import run_bass_kernel_spmd

    def attention(name):
        return inputs["L0_xattn_" + name]

    def ffn(name):
        return inputs["L0_ffn_" + name]

    gate = np.concatenate([ffn("sw_gate")[None], ffn("w_gate")])
    up = np.concatenate([ffn("sw_up")[None], ffn("w_up")])
    down = np.concatenate([ffn("sw_down")[None], ffn("w_down")])
    gate_up = np.concatenate([gate, up], axis=2).reshape(EXPERTS + 1, CHUNKS, P, 2 * FF)
    weights = np.concatenate([gate_up, down.reshape(EXPERTS + 1, FF // P, P, L)], axis=1)
    x = inputs["x"]
    arrays = dict(
        x=x, ctx=inputs["ctx_2048"], g_xattn=inputs["g_xattn"].reshape(1, 1), g_ffn=inputs["g_ffn"].reshape(1, 1),
        wq=attention("Wq").T, bq=attention("bq").reshape(P, 1), wk=attention("Wk").T, bk=attention("bk").reshape(P, 1),
        wv=attention("Wv").T, bv=attention("bv").reshape(P, 1), rms=ffn("rms_weight").reshape(1, L),
        router=ffn("router_w"), w=weights.transpose(0, 2, 1, 3))
    arrays = {f"in_{name}": np.ascontiguousarray(value) for name, value in arrays.items()}
    tokens = x.shape[0] * P
    nc = bacc.Bacc("TRN2", target_bir_lowering=False, num_devices=1)
    tensors = [nc.dram_tensor(name, value.shape, mybir.dt.from_np(value.dtype), kind="ExternalInput").ap()
               for name, value in arrays.items()]
    tensors.append(nc.dram_tensor("out", (tokens + P, L), F32, kind="ExternalOutput").ap())
    build(nc, *tensors)
    result = run_bass_kernel_spmd(nc, [arrays], core_ids=[0]).results[0]["out"]
    return result[:tokens].reshape(x.shape)
```
